# Optimizing a Trainium2 kernel written in Bass

```python
import numpy as np
import jax
import jax.numpy as jnp

def _softmax(x, axis=-1):
    return jax.nn.softmax(x, axis=axis)

def _gelu(x):
    return jax.nn.gelu(x, approximate=True)

def _silu(x):
    return jax.nn.silu(x)

def _sigmoid(x):
    return jax.nn.sigmoid(x)

def _layernorm(x, axis=-1, eps=1e-05):
    m = jnp.mean(x, axis=axis, keepdims=True)
    v = jnp.var(x, axis=axis, keepdims=True)
    return (x - m) / jnp.sqrt(v + eps)

def _scatter_add(tgt, idx, src, axis=0):
    return tgt.at[idx].add(src)

def _segment_sum(src, seg, n):
    return jax.ops.segment_sum(src, seg, n)
kernel_name = 'mk_audio_tower_d2_tok_audfeat256_r4_ff097e'

def setup_inputs(seed: int=0):
    np.random.seed(seed)
    _w = jnp.asarray

    def _rec_inputs():
        import jax
        import jax.numpy as jnp
        _rk = jax.random.key(seed)
        x = jax.random.uniform(jax.random.fold_in(_rk, 1), (16, 4, 256), jnp.float32, 0.0, 0.999986)
        return x
    x = _rec_inputs()

    def _L0_tok_setup():
        import jax, jax.numpy as jnp
        import numpy as np
        T = 8
        key = jax.random.key(seed)
        ks = jax.random.split(key, 9)
        bs, dims, L, d = (16, 4, 512, 64)
        x = jax.random.uniform(ks[0], (bs, dims, L), dtype=jnp.float32)
        s_in = 1.0 / np.sqrt(dims)
        s_d = 1.0 / np.sqrt(d)
        W1 = jax.random.uniform(ks[1], (d, dims), minval=-s_in, maxval=s_in, dtype=jnp.float32)
        b1 = jax.random.uniform(ks[2], (d,), minval=-s_in, maxval=s_in, dtype=jnp.float32)
        W2 = jax.random.uniform(ks[3], (d, d), minval=-s_d, maxval=s_d, dtype=jnp.float32)
        b2 = jax.random.uniform(ks[4], (d,), minval=-s_d, maxval=s_d, dtype=jnp.float32)
        W3 = jax.random.uniform(ks[5], (d, dims), minval=-s_in, maxval=s_in, dtype=jnp.float32)
        b3 = jax.random.uniform(ks[6], (d,), minval=-s_in, maxval=s_in, dtype=jnp.float32)
        W4 = jax.random.uniform(ks[7], (d, d), minval=-s_d, maxval=s_d, dtype=jnp.float32)
        b4 = jax.random.uniform(ks[8], (d,), minval=-s_d, maxval=s_d, dtype=jnp.float32)
        return dict(x=x, W1=W1, b1=b1, W2=W2, b2=b2, W3=W3, b3=b3, W4=W4, b4=b4)
    _L0_tok_all = _L0_tok_setup()
    _L0_tok_in = {k: v for k, v in _L0_tok_all.items() if k in ('W1', 'b1', 'W2', 'b2', 'W3', 'b3', 'W4', 'b4')}
    del _L0_tok_all

    def _L0_attn_setup():
        import jax, jax.numpy as jnp
        import numpy as np
        D_ATT = 64
        D_GROUP = 32
        N_GROUP = D_ATT // D_GROUP
        key = jax.random.key(seed)
        ks = jax.random.split(key, 6)
        B, L = (4, 128)
        import math
        s = 1.0 / math.sqrt(D_ATT)
        return {'x': jax.random.normal(ks[0], (B, L, D_ATT), dtype=jnp.float32), 'Wq': jax.random.normal(ks[1], (D_ATT, D_ATT), dtype=jnp.float32) * s * 0.06, 'Wk': jax.random.normal(ks[2], (D_ATT, D_ATT), dtype=jnp.float32) * s * 0.06, 'Wv': jax.random.normal(ks[3], (D_ATT, D_ATT), dtype=jnp.float32) * s * 0.06, 'w_mlp': jax.random.normal(ks[4], (D_GROUP,), dtype=jnp.float32) * 0.1, 'b_mlp': jax.random.normal(ks[5], (1,), dtype=jnp.float32) * 0.1}
    _L0_attn_all = _L0_attn_setup()
    _L0_attn_in = {k: v for k, v in _L0_attn_all.items() if k in ('Wq', 'Wk', 'Wv', 'w_mlp', 'b_mlp')}
    del _L0_attn_all

    def _L0_ffn_setup():
        import jax, jax.numpy as jnp
        import numpy as np
        NUM_EXPERTS = 8
        TOP_K = 2
        B, S, D = (8, 2048, 64)

        def _moe(tokens, router_w, w1, b1, w2, b2):
            N = tokens.shape[0]
            E = router_w.shape[0]
            logits = tokens.astype(jnp.float32) @ router_w.astype(jnp.float32).T
            probs = jax.nn.softmax(logits, axis=-1)
            rw, re = jax.lax.top_k(probs, TOP_K)
            if TOP_K > 1:
                rw = rw / jnp.maximum(rw.sum(-1, keepdims=True), 1e-12)
            rw = rw.astype(tokens.dtype)
            combine = jnp.zeros((N, E), tokens.dtype).at[jnp.arange(N)[:, None], re].set(rw)
            out = tokens
            for e in range(E):
                h = jax.nn.gelu(tokens @ w1[e] + b1[e], approximate=False)
                y = h @ w2[e] + b2[e]
                out = out + combine[:, e:e + 1] * y
            return out
        key = jax.random.key(seed)
        ks = jax.random.split(key, 4)
        scale = 1.0 / np.sqrt(D).astype(np.float32)
        return {'input_embeddings': jax.random.normal(ks[0], (B, S, D), jnp.float32), 'router_w': jax.random.normal(ks[1], (NUM_EXPERTS, D), jnp.float32) * scale, 'w1': jax.random.normal(ks[2], (NUM_EXPERTS, D, D), jnp.float32) * scale, 'b1': jnp.zeros((NUM_EXPERTS, D), jnp.float32), 'w2': jax.random.normal(ks[3], (NUM_EXPERTS, D, D), jnp.float32) * scale, 'b2': jnp.zeros((NUM_EXPERTS, D), jnp.float32)}
    _L0_ffn_all = _L0_ffn_setup()
    _L0_ffn_in = {k: v for k, v in _L0_ffn_all.items() if k in ('router_w', 'w1', 'b1', 'w2', 'b2')}
    del _L0_ffn_all

    def _L1_attn_setup():
        import jax, jax.numpy as jnp
        import numpy as np
        B, T, C = (16, 512, 64)
        TT = T
        LAYER_ID, N_LAYER = (3, 6)
        key = jax.random.key(seed)
        ks = jax.random.split(key, 6)
        ratio_0_to_1 = LAYER_ID / (N_LAYER - 1)
        ratio_1_to_almost0 = 1.0 - LAYER_ID / N_LAYER
        h = np.arange(TT, dtype=np.float32)
        decay_speed = -5.0 + 8.0 * (h / (TT - 1)) ** (0.7 + 1.3 * ratio_0_to_1)
        curve = -(TT - 1 - h)
        time_w = jnp.asarray(np.exp(np.clip(curve * decay_speed, -30.0, 0.0)), dtype=jnp.float32)
        i = np.arange(C, dtype=np.float32) / C
        time_mix_k = jnp.asarray((i ** ratio_1_to_almost0).reshape(1, 1, C), dtype=jnp.float32)
        time_mix_v = jnp.asarray((i ** ratio_1_to_almost0 + 0.3 * ratio_0_to_1).reshape(1, 1, C), dtype=jnp.float32)
        time_mix_r = jnp.asarray((i ** (0.5 * ratio_1_to_almost0)).reshape(1, 1, C), dtype=jnp.float32)
        x = jax.random.normal(ks[0], (B, T, C), dtype=jnp.float32)
        scale = 0.02
        Wk = scale * jax.random.normal(ks[1], (C, C), dtype=jnp.float32)
        Wv = scale * jax.random.normal(ks[2], (C, C), dtype=jnp.float32)
        Wr = scale * jax.random.normal(ks[3], (C, C), dtype=jnp.float32)
        Wo = scale * jax.random.normal(ks[4], (C, C), dtype=jnp.float32)
        return {'x': x, 'time_w': time_w, 'time_mix_k': time_mix_k, 'time_mix_v': time_mix_v, 'time_mix_r': time_mix_r, 'Wk': Wk, 'Wv': Wv, 'Wr': Wr, 'Wo': Wo}
    _L1_attn_all = _L1_attn_setup()
    _L1_attn_in = {k: v for k, v in _L1_attn_all.items() if k in ('time_w', 'time_mix_k', 'time_mix_v', 'time_mix_r', 'Wk', 'Wv', 'Wr', 'Wo')}
    del _L1_attn_all

    def _L1_ffn_setup():
        import jax, jax.numpy as jnp
        import numpy as np
        B, N, D = (16, 1024, 64)
        NUM_EXPERTS, TOP_K, HEADS = (4, 2, 4)
        N_EDGES = 262144
        LN_EPS = 1e-05

        def _layernorm(x, g, b):
            mu = x.mean(-1, keepdims=True)
            var = ((x - mu) ** 2).mean(-1, keepdims=True)
            return (x - mu) * jax.lax.rsqrt(var + LN_EPS) * g + b

        def _forward(x, edge_index, W_gat, att_src, att_dst, b_gat, ln_gamma, ln_beta, W1, b1, W2, b2):
            Bc, Nc, Dc = x.shape
            M = Bc * Nc
            x_flat = x.reshape(M, Dc)
            h = (x_flat @ W_gat).reshape(M, HEADS, NUM_EXPERTS)
            loops = jnp.arange(M, dtype=edge_index.dtype)
            src = jnp.concatenate([edge_index[0], loops])
            dst = jnp.concatenate([edge_index[1], loops])
            a_src = (h * att_src).sum(-1)
            a_dst = (h * att_dst).sum(-1)
            e = jax.nn.leaky_relu(a_src[src] + a_dst[dst], negative_slope=0.2)
            e_max = jax.ops.segment_max(e, dst, num_segments=M)
            ee = jnp.exp(e - e_max[dst])
            denom = jax.ops.segment_sum(ee, dst, num_segments=M)
            alpha = ee / (denom[dst] + 1e-16)
            msg = h[src] * alpha[:, :, None]
            agg = jax.ops.segment_sum(msg, dst, num_segments=M).reshape(M, HEADS * NUM_EXPERTS) + b_gat
            scores = _layernorm(agg, ln_gamma, ln_beta).reshape(M, HEADS, NUM_EXPERTS).mean(1)
            scores = scores.reshape(Bc, Nc, NUM_EXPERTS)
            topk_s, topk_i = jax.lax.top_k(scores, TOP_K)
            w = jax.nn.softmax(topk_s, axis=-1)
            out = jnp.zeros_like(x)
            for ei in range(NUM_EXPERTS):
                g = jnp.where(topk_i == ei, w, 0.0).sum(-1)
                hh = jax.nn.gelu(x @ W1[ei] + b1[ei], approximate=False)
                out = out + g[..., None] * (hh @ W2[ei] + b2[ei])
            return out
        key = jax.random.key(seed)
        ks = jax.random.split(key, 8)
        s = 0.05
        return {'x': jax.random.normal(ks[0], (B, N, D), jnp.float32), 'W_gat': jax.random.normal(ks[1], (D, HEADS * NUM_EXPERTS), jnp.float32) * s, 'att_src': jax.random.normal(ks[2], (HEADS, NUM_EXPERTS), jnp.float32) * s, 'att_dst': jax.random.normal(ks[3], (HEADS, NUM_EXPERTS), jnp.float32) * s, 'b_gat': jnp.zeros((HEADS * NUM_EXPERTS,), jnp.float32), 'ln_gamma': jnp.ones((HEADS * NUM_EXPERTS,), jnp.float32), 'ln_beta': jnp.zeros((HEADS * NUM_EXPERTS,), jnp.float32), 'W1': jax.random.normal(ks[4], (NUM_EXPERTS, D, 2 * D), jnp.float32) * s, 'b1': jnp.zeros((NUM_EXPERTS, 2 * D), jnp.float32), 'W2': jax.random.normal(ks[5], (NUM_EXPERTS, 2 * D, D), jnp.float32) * s, 'b2': jnp.zeros((NUM_EXPERTS, D), jnp.float32), 'edge_index': jax.random.randint(ks[6], (2, N_EDGES), 0, B * N, jnp.int32)}
    _L1_ffn_all = _L1_ffn_setup()
    _L1_ffn_in = {k: v for k, v in _L1_ffn_all.items() if k in ('W_gat', 'att_src', 'att_dst', 'b_gat', 'ln_gamma', 'ln_beta', 'W1', 'b1', 'W2', 'b2', 'edge_index')}
    del _L1_ffn_all
    return {'x': x, 'L0_tok_W1': _L0_tok_in['W1'], 'L0_tok_b1': _L0_tok_in['b1'], 'L0_tok_W2': _L0_tok_in['W2'], 'L0_tok_b2': _L0_tok_in['b2'], 'L0_tok_W3': _L0_tok_in['W3'], 'L0_tok_b3': _L0_tok_in['b3'], 'L0_tok_W4': _L0_tok_in['W4'], 'L0_tok_b4': _L0_tok_in['b4'], 'L0_attn_Wq': _L0_attn_in['Wq'], 'L0_attn_Wk': _L0_attn_in['Wk'], 'L0_attn_Wv': _L0_attn_in['Wv'], 'L0_attn_w_mlp': _L0_attn_in['w_mlp'], 'L0_attn_b_mlp': _L0_attn_in['b_mlp'], 'L0_ffn_router_w': _L0_ffn_in['router_w'], 'L0_ffn_w1': _L0_ffn_in['w1'], 'L0_ffn_b1': _L0_ffn_in['b1'], 'L0_ffn_w2': _L0_ffn_in['w2'], 'L0_ffn_b2': _L0_ffn_in['b2'], 'L1_attn_time_w': _L1_attn_in['time_w'], 'L1_attn_time_mix_k': _L1_attn_in['time_mix_k'], 'L1_attn_time_mix_v': _L1_attn_in['time_mix_v'], 'L1_attn_time_mix_r': _L1_attn_in['time_mix_r'], 'L1_attn_Wk': _L1_attn_in['Wk'], 'L1_attn_Wv': _L1_attn_in['Wv'], 'L1_attn_Wr': _L1_attn_in['Wr'], 'L1_attn_Wo': _L1_attn_in['Wo'], 'L1_ffn_W_gat': _L1_ffn_in['W_gat'], 'L1_ffn_att_src': _L1_ffn_in['att_src'], 'L1_ffn_att_dst': _L1_ffn_in['att_dst'], 'L1_ffn_b_gat': _L1_ffn_in['b_gat'], 'L1_ffn_ln_gamma': _L1_ffn_in['ln_gamma'], 'L1_ffn_ln_beta': _L1_ffn_in['ln_beta'], 'L1_ffn_W1': _L1_ffn_in['W1'], 'L1_ffn_b1': _L1_ffn_in['b1'], 'L1_ffn_W2': _L1_ffn_in['W2'], 'L1_ffn_b2': _L1_ffn_in['b2'], 'L1_ffn_edge_index': _L1_ffn_in['edge_index']}

def reference(x, L0_tok_W1, L0_tok_b1, L0_tok_W2, L0_tok_b2, L0_tok_W3, L0_tok_b3, L0_tok_W4, L0_tok_b4, L0_attn_Wq, L0_attn_Wk, L0_attn_Wv, L0_attn_w_mlp, L0_attn_b_mlp, L0_ffn_router_w, L0_ffn_w1, L0_ffn_b1, L0_ffn_w2, L0_ffn_b2, L1_attn_time_w, L1_attn_time_mix_k, L1_attn_time_mix_v, L1_attn_time_mix_r, L1_attn_Wk, L1_attn_Wv, L1_attn_Wr, L1_attn_Wo, L1_ffn_W_gat, L1_ffn_att_src, L1_ffn_att_dst, L1_ffn_b_gat, L1_ffn_ln_gamma, L1_ffn_ln_beta, L1_ffn_W1, L1_ffn_b1, L1_ffn_W2, L1_ffn_b2, L1_ffn_edge_index):
    import jax
    import jax.numpy as jnp

    def _L0_tok_ref(x, W1, b1, W2, b2, W3, b3, W4, b4):
        import jax, jax.numpy as jnp
        import numpy as np
        T = 8
        a = jnp.einsum('bdl,od->blo', x, W1) + b1
        bs, L, d = a.shape
        zcol = jnp.zeros((bs, 1, d), a.dtype)
        shift_r = lambda v: jnp.concatenate([zcol, v[:, :-1]], axis=1)
        shift_l = lambda v: jnp.concatenate([v[:, 1:], zcol], axis=1)
        up = jnp.zeros_like(a)
        down = jnp.zeros_like(a)
        for _ in range(T):
            up = jax.nn.relu(a + shift_r(up) @ W2.T + b2)
            down = jax.nn.relu(a + shift_l(down) @ W2.T + b2)
        c = jnp.einsum('bdl,od->blo', x, W3) + b3
        miu = jax.nn.relu(c + (shift_r(up) @ W4.T + b4) + (shift_l(down) @ W4.T + b4))
        return miu

    def _L0_attn_ref(x, Wq, Wk, Wv, w_mlp, b_mlp):
        import jax, jax.numpy as jnp
        import numpy as np
        D_ATT = 64
        D_GROUP = 32
        N_GROUP = D_ATT // D_GROUP
        B, L, d_att = x.shape
        G, Dg = (N_GROUP, D_GROUP)
        Q = x @ Wq.T
        K = x @ Wk.T
        V = x @ Wv.T
        Qg = Q.reshape(B, L, 1, G, Dg)
        Kg = K.reshape(B, 1, L, G, Dg)
        diff = Qg - Kg
        attn = jnp.einsum('bqkgd,d->bqkg', jax.nn.relu(diff), w_mlp) + b_mlp[0]
        attn = jax.nn.relu(attn)
        attn = jax.nn.softmax(attn, axis=2)
        Vg = V.reshape(B, L, Dg, G)
        out = jnp.einsum('bqkg,bkdg->bqdg', attn, Vg)
        return out.reshape(B, L, d_att)

    def _L0_ffn_ref(input_embeddings, router_w, w1, b1, w2, b2):
        import jax, jax.numpy as jnp
        import numpy as np
        NUM_EXPERTS = 8
        TOP_K = 2
        B, S, D = (8, 2048, 64)

        def _moe(tokens, router_w, w1, b1, w2, b2):
            N = tokens.shape[0]
            E = router_w.shape[0]
            logits = tokens.astype(jnp.float32) @ router_w.astype(jnp.float32).T
            probs = jax.nn.softmax(logits, axis=-1)
            rw, re = jax.lax.top_k(probs, TOP_K)
            if TOP_K > 1:
                rw = rw / jnp.maximum(rw.sum(-1, keepdims=True), 1e-12)
            rw = rw.astype(tokens.dtype)
            combine = jnp.zeros((N, E), tokens.dtype).at[jnp.arange(N)[:, None], re].set(rw)
            out = tokens
            for e in range(E):
                h = jax.nn.gelu(tokens @ w1[e] + b1[e], approximate=False)
                y = h @ w2[e] + b2[e]
                out = out + combine[:, e:e + 1] * y
            return out
        b, s, d = input_embeddings.shape
        tokens = input_embeddings.reshape(b * s, d)
        return _moe(tokens, router_w, w1, b1, w2, b2).reshape(b, s, d)

    def _L1_attn_ref(x, time_w, time_mix_k, time_mix_v, time_mix_r, Wk, Wv, Wr, Wo):
        import jax, jax.numpy as jnp
        import numpy as np
        B, T, C = (16, 512, 64)
        TT = T
        LAYER_ID, N_LAYER = (3, 6)
        Bx, Tx, Cx = x.shape
        maxlen = time_w.shape[0]
        xx = jnp.pad(x, ((0, 0), (1, 0), (0, 0)))[:, :-1]
        xk = x * time_mix_k + xx * (1.0 - time_mix_k)
        xv = x * time_mix_v + xx * (1.0 - time_mix_v)
        xr = x * time_mix_r + xx * (1.0 - time_mix_r)
        k = jnp.exp(jnp.clip(xk @ Wk, -60.0, 30.0))
        v = xv @ Wv
        r = xr @ Wr
        sum_k = jnp.cumsum(k, axis=1)
        kv = k * v
        t_idx = jnp.arange(Tx)
        d = t_idx[:, None] - t_idx[None, :]
        W = jnp.where(d >= 0, time_w[jnp.clip(maxlen - 1 - d, 0, maxlen - 1)], 0.0)
        wkv = jnp.einsum('tu,buc->btc', W, kv)
        rwkv = jax.nn.sigmoid(r) * wkv / sum_k
        return rwkv @ Wo

    def _L1_ffn_ref(x, W_gat, att_src, att_dst, b_gat, ln_gamma, ln_beta, W1, b1, W2, b2, edge_index):
        import jax, jax.numpy as jnp
        import numpy as np
        B, N, D = (16, 1024, 64)
        NUM_EXPERTS, TOP_K, HEADS = (4, 2, 4)
        N_EDGES = 262144
        LN_EPS = 1e-05

        def _layernorm(x, g, b):
            mu = x.mean(-1, keepdims=True)
            var = ((x - mu) ** 2).mean(-1, keepdims=True)
            return (x - mu) * jax.lax.rsqrt(var + LN_EPS) * g + b

        def _forward(x, edge_index, W_gat, att_src, att_dst, b_gat, ln_gamma, ln_beta, W1, b1, W2, b2):
            Bc, Nc, Dc = x.shape
            M = Bc * Nc
            x_flat = x.reshape(M, Dc)
            h = (x_flat @ W_gat).reshape(M, HEADS, NUM_EXPERTS)
            loops = jnp.arange(M, dtype=edge_index.dtype)
            src = jnp.concatenate([edge_index[0], loops])
            dst = jnp.concatenate([edge_index[1], loops])
            a_src = (h * att_src).sum(-1)
            a_dst = (h * att_dst).sum(-1)
            e = jax.nn.leaky_relu(a_src[src] + a_dst[dst], negative_slope=0.2)
            e_max = jax.ops.segment_max(e, dst, num_segments=M)
            ee = jnp.exp(e - e_max[dst])
            denom = jax.ops.segment_sum(ee, dst, num_segments=M)
            alpha = ee / (denom[dst] + 1e-16)
            msg = h[src] * alpha[:, :, None]
            agg = jax.ops.segment_sum(msg, dst, num_segments=M).reshape(M, HEADS * NUM_EXPERTS) + b_gat
            scores = _layernorm(agg, ln_gamma, ln_beta).reshape(M, HEADS, NUM_EXPERTS).mean(1)
            scores = scores.reshape(Bc, Nc, NUM_EXPERTS)
            topk_s, topk_i = jax.lax.top_k(scores, TOP_K)
            w = jax.nn.softmax(topk_s, axis=-1)
            out = jnp.zeros_like(x)
            for ei in range(NUM_EXPERTS):
                g = jnp.where(topk_i == ei, w, 0.0).sum(-1)
                hh = jax.nn.gelu(x @ W1[ei] + b1[ei], approximate=False)
                out = out + g[..., None] * (hh @ W2[ei] + b2[ei])
            return out
        return _forward(x, edge_index, W_gat, att_src, att_dst, b_gat, ln_gamma, ln_beta, W1, b1, W2, b2)
    h = _L0_tok_ref(x, L0_tok_W1, L0_tok_b1, L0_tok_W2, L0_tok_b2, L0_tok_W3, L0_tok_b3, L0_tok_W4, L0_tok_b4)
    h = h + _L0_attn_ref(_layernorm(h, axis=-1), L0_attn_Wq, L0_attn_Wk, L0_attn_Wv, L0_attn_w_mlp, L0_attn_b_mlp)
    h = h + _L0_ffn_ref(_layernorm(h, axis=-1), L0_ffn_router_w, L0_ffn_w1, L0_ffn_b1, L0_ffn_w2, L0_ffn_b2)
    h = h + _L1_attn_ref(_layernorm(h, axis=-1), L1_attn_time_w, L1_attn_time_mix_k, L1_attn_time_mix_v, L1_attn_time_mix_r, L1_attn_Wk, L1_attn_Wv, L1_attn_Wr, L1_attn_Wo)
    h = h + _L1_ffn_ref(_layernorm(h, axis=-1), L1_ffn_W_gat, L1_ffn_att_src, L1_ffn_att_dst, L1_ffn_b_gat, L1_ffn_ln_gamma, L1_ffn_ln_beta, L1_ffn_W1, L1_ffn_b1, L1_ffn_W2, L1_ffn_b2, L1_ffn_edge_index)
    return h

_drawn_inputs = setup_inputs


def setup_inputs(seed=0):
    import zlib

    import numpy as np

    out = dict(_drawn_inputs(seed))
    spreads = {'L0_ffn_b1': (0.0, 0.1),
     'L0_ffn_b2': (0.0, 0.1),
     'L1_ffn_b_gat': (0.0, 1.982),
     'L1_ffn_ln_gamma': (1.0, 0.6),
     'L1_ffn_ln_beta': (0.0, 2.0),
     'L1_ffn_b1': (0.0, 2.0),
     'L1_ffn_b2': (0.0, 0.8)}
    factors = {'L0_attn_Wq': 8.0,
     'L0_attn_Wk': 8.0,
     'L0_attn_w_mlp': 8.0,
     'L1_attn_time_w': 8.0,
     'L1_attn_time_mix_k': 8.0,
     'L1_attn_time_mix_v': 8.0,
     'L1_attn_time_mix_r': 8.0,
     'L1_attn_Wk': 8.0,
     'L1_attn_Wv': 8.0,
     'L1_attn_Wr': 8.0,
     'L1_attn_Wo': 8.0,
     'L1_ffn_att_src': 64.0,
     'L1_ffn_att_dst': 64.0,
     'L1_ffn_W_gat': 8.0,
     'L1_ffn_W1': 8.0,
     'L1_ffn_W2': 5.669}
    for name, (base, spread) in spreads.items():
        noise = np.random.default_rng([zlib.crc32(name.encode()), seed]).standard_normal(out[name].shape)
        drawn = base * np.exp(spread * noise) if base else spread * noise
        out[name] = jnp.asarray(drawn.astype(out[name].dtype))
    for name, factor in factors.items():
        out[name] = (out[name] * factor).astype(out[name].dtype)
    return out
```

```python
import concourse.bass as bass
from concourse import mybir
from contextlib import ExitStack

P = 128
UPTO = 4


def audio_tower(nc, t):
    f32 = mybir.dt.float32
    ALU = mybir.AluOpType
    ACT = mybir.ActivationFunctionType
    AX = mybir.AxisListType
    ds = bass.ds

    NB, L, D = 8, 256, 64
    COLS = NB * L
    CH = 512
    NCH = COLS // CH
    TILES = COLS // P
    STEPS = 8
    G = 2
    NG = 2 * G
    QT = 32
    TPP = L // QT
    NR = 16
    E = 8
    EPS = 1e-5
    BIG = 1e30
    E1, HEADS = 4, 4
    f16, i32 = mybir.dt.float16, mybir.dt.int32
    NE = 262144
    EPP = NE // P
    GEN = EPP
    M = 4096
    NQ = M // P
    HT = 64
    XC = 104
    XT = 2 * XC
    WL = 192
    GR, GS = 4, 64
    QG = NQ // GR
    ARENA = 35600
    K_MAX, K_SUM = 26, 20

    ctx = ExitStack()
    with ctx:
        def sb(name, shape, dt=f32):
            return ctx.enter_context(nc.sbuf_tensor(name, shape, dt))

        def sem(name):
            return ctx.enter_context(nc.semaphore(name))

        ps = ctx.enter_context(nc.psum_tensor("ps", [P, 8, CH], f32))

        arena = sb("arena", [P, ARENA])
        off = [0]

        def carve(shape, dt=f32):
            n = 1
            for d in shape:
                n *= d
            words = n * (2 if dt == f16 else 4) // 4
            a = arena[:, off[0]:off[0] + words]
            off[0] += words
            assert off[0] <= ARENA, off[0]
            a = a if dt == f32 else a.bitcast(dt)
            names = "abcd"[:len(shape)]
            if len(shape) > 1:
                a = a.rearrange("p (%s) -> p %s" % (" ".join(names), " ".join(names)), **dict(zip(names, shape)))
            return a

        h, dev, sq, nrm = [carve([COLS]) for _ in range(4)]
        x_sb = carve([COLS])[0:8]
        wt_sb = sb("wt_sb", [8, 2 * P])
        w_sb = sb("w_sb", [P, t["wmat"].shape[1]])
        c_sb = sb("c_sb", [P, t["cols"].shape[1]])
        slide = sb("slide", [P, 60])
        eye = sb("eye", [P, P])
        dyn = sb("dyn", [P, 8])
        a_sb = carve([COLS])
        up = carve([2, NB, L + 2])
        dn = carve([2, NB, L + 2])
        q_sb = a_sb
        k_sb = dn[:, :, :, :].rearrange("p a b l -> p (a b l)")[:, 0:COLS]
        nq_sb, nk_sb = dev, sq
        v_sb = carve([TILES, P])
        relu = carve([NR, L])
        sc = sb("sc", [P, 2, L])
        st = sb("st", [P, 2, 4])
        vp = sb("vp", [P, 2, P])
        pT = sb("pT", [P, 2, 2, P])
        ao = sb("ao", [P, P])
        router = sb("router", [P, 16])
        moe_w = sb("moe_w", [P, 2, E, P])
        moe_b2 = sb("moe_b2", [16, P])
        pick = sb("pick", [16, E, P])
        rank_w = sb("rank_w", [P, E])
        lg, eq, s1, l2, s2 = [carve([2 * TILES, E]) for _ in range(5)]
        m1, mr = sb("m1", [P, 2 * TILES]), sb("mr", [P, 2 * TILES])
        cmbF = carve([COLS])[0:16]
        gbuf = carve([2, CH])
        gs = carve([2, CH])
        rk_raw = sb("rk_raw", [P, 3, P])
        rk_w = sb("rk_w", [P, 2, 3, P])
        wo_sb = sb("wo_sb", [P, P])
        omix = sb("omix", [P, 3])
        tw = sb("tw", [P, 2, L])
        tri = sb("tri", [P, 2, L])
        kT = carve([2, 2, P])
        kvT = carve([2, 2, P])
        sig = v_sb[:, :, :].rearrange("p t f -> p (t f)")
        rw = carve([2, 2, L])
        off[0] = 4 * COLS
        hg, num, gtmp = [carve([NQ, 16]) for _ in range(3)]
        a_self, a_dst, a_top, a_y, den, e_self, e_alias, aliased = [carve([NQ, HEADS]) for _ in range(8)]
        e_small = carve([2, NQ, HEADS])
        pen, mu, rstd = [carve([NQ]) for _ in range(3)]
        hc, hct = carve([16]), carve([16])
        a_c = carve([HEADS])
        gath = carve([GR * GS, 16])
        g_src = carve([GR * GS, HEADS])
        g_tmp = carve([GS, 16])
        pn = carve([GR, QG, GS])
        T1_AT = [off[0]]
        t1 = carve([HEADS, QG, GS])
        t2 = carve([4, QG, GS])
        g_top = carve([HEADS, QG])
        yb = carve([2 * TILES * E1, D])
        g1 = carve([2, CH])
        tl, te, t_1, t_l2, t_2 = [carve([2 * TILES, E1]) for _ in range(5)]
        tm1, tmr = carve([2 * TILES]), carve([2 * TILES])
        g2 = carve([2 * TILES, E1])
        outY = carve([TILES, 2, D])
        c_mask = gath.rearrange("p w f -> p (w f)").rearrange("p (q e) -> p q e", q=NQ)
        assert GS * GR * 16 == NQ * P
        c_pick = arena[:, T1_AT[0]:T1_AT[0] + NQ * P].rearrange("p (q e) -> p q e", q=NQ)
        c_diag = outY.rearrange("p t h f -> p (t h f)")[:, 0:6 * P].rearrange("p (r e) -> p r e", r=6)
        c_rhs = outY.rearrange("p t h f -> p (t h f)")[:, 6 * P:6 * P + NQ * 20].rearrange("p (q v) -> p q v", q=NQ)
        c_hot = outY.rearrange("p t h f -> p (t h f)")[:, 6 * P + NQ * 20:7 * P + NQ * 20]
        off[0] = 0
        e_src, e_dst = carve([EPP], i32), carve([EPP], i32)
        e_lo, e_q = carve([EPP], i32), carve([EPP], i32)
        e_key, e_tmp = carve([EPP]), carve([EPP])
        d_lo, d_hi = carve([EPP], f16), carve([EPP], f16)
        iota_x = carve([64, HT], f16)
        hot_lo = [carve([64, HT], f16) for _ in range(2)]
        hot_hi = [carve([64, HT], f16) for _ in range(2)]
        off[0] = 6 * EPP
        hot = carve([XT, P], f16)
        hot_off = carve([XT // 8, P])
        off[0] = 0
        slot_hot = [carve([2, WL], f16) for _ in range(4)]
        x_key = carve([XT])
        x_i, x_b, x_t1, x_t2 = [carve([XT], i32) for _ in range(4)]
        x_bf, x_A, x_B, x_new, x_run, x_rank, x_zero = [carve([XT]) for _ in range(7)]
        cnt_sb = carve([2, P], f16)
        off_sb = carve([2, P])
        l_key, l_g, l_m = carve([WL]), carve([WL]), carve([WL])
        l_i = carve([GR * GS], i32)
        assert off[0] <= 6 * EPP
        w_gat = sb("w_gat", [P, 32])
        grow = sb("grow", [P, 5, 16])
        w1s = sb("w1s", [P, E1, P])
        w2s = sb("w2s", [P, E1, D])
        f_b1 = sb("f_b1", [P, E1])
        b2r = sb("b2r", [1, E1, D])
        ones1 = sb("ones1", [1, P])
        table = nc.dram_tensor("gat_table", (M, 16), f32, kind="Internal").ap()
        q1f = sb("q1f", [P, GR * GS])
        table2 = nc.dram_tensor("gat_dst_table", (M, 8), f32, kind="Internal").ap()
        ones_sq = sb("ones_sq", [P, P])
        lane_id = sb("lane_id", [P, 1])
        idxQ = sb("idxQ", [P, NQ])
        flag = sb("flag", [P, 2])
        flag_i = sb("flag_i", [1, 1], i32)
        c_src, c_dst, c_lo, c_q, c_si, c_di = [sb(n, [P, 1], i32) for n in ("c_src", "c_dst", "c_lo", "c_q", "c_si", "c_di")]
        c_g, c_d = sb("c_g", [P, 16]), sb("c_d", [P, 8])
        c_f = sb("c_f", [P, 4])
        c_v = sb("c_v", [P, 6])
        c_t = sb("c_t", [P, 16])
        c_w = sb("c_w", [P, 2])
        c_e = sb("c_e", [P, 20])
        c_row = sb("c_row", [P, 2, P])
        c_top = sb("c_top", [P, NQ])
        c_tab = sb("c_tab", [P, NQ, 8])
        idx128 = sb("idx128", [P, P], f16)
        idxW = sb("idxW", [P, WL], f16)
        idxXT = sb("idxXT", [P, XT])
        cst = sb("cst", [P, 4, P], f16)
        half_f = sb("half_f", [P, 2, P])
        hsb = sb("hsb", [64, 64])
        nd = sb("nd", [P, NQ])
        s_key = sb("s_key", [P, GR, GS])
        s_idx = sb("s_idx", [P, GR * GS], i32)
        bad = sb("bad", [P, 4])
        outT = k_sb.rearrange("p (t h f) -> p t h f", t=TILES, h=2)

        W = {n: w_sb[:, i * P:(i + 1) * P] for i, n in enumerate(
            ["tok2", "tok4", "q", "k", "v", "mean"])}
        C = {n: c_sb[:, i:i + 1] for i, n in enumerate(["b1", "b2", "b3", "b4", "b_mlp", "mixk", "mixv", "mixr"] + ["moe_b1_%d" % e for e in range(E)])}

        s_w = sem("weights_loaded")
        s_c = sem("edge_constants_loaded")
        s_x = sem("x_loaded")
        dve_done = sem("dve_done")
        recip_done = sem("recip_done")
        vp_ready = sem("vp_ready")
        bias_ready, tok_a, tok_mm, tok_sum, tok_relu, tok_out_mm, h_tok = [sem(n) for n in (
            "bias_ready", "tok_a", "tok_mm", "tok_sum", "tok_relu", "tok_out_mm", "h_tok")]
        ln_mean, ln_dev, ln_sq, ln_var, ln_std, ln_out = [
            sem("ln_" + n) for n in ("mean", "dev", "sq", "var", "std", "out")]
        qk_mm, qk_copied, v_mm, v_copied = sem("qk_mm"), sem("qk_copied"), sem("v_mm"), sem("v_copied")
        relu_dve, relu_act, relu_used = sem("relu_dve"), sem("relu_act"), sem("relu_used")
        score_mm, score_read, max_ready, exp_ready, prob_ready = [sem(n) for n in (
            "score_mm", "score_read", "max_ready", "exp_ready", "prob_ready")]
        prob_T, pT_copied, pv_mm, ao_copied, ao_T, h_attn = [sem(n) for n in (
            "prob_T", "pT_copied", "pv_mm", "ao_copied", "ao_T", "h_attn")]
        lg_mm, ex_in, ex_done, cmb_ready, cmb_T, cmb_copied = [sem(n) for n in (
            "lg_mm", "ex_in", "ex_done", "cmb_ready", "cmb_T", "cmb_copied")]
        moe_hid, moe_bc, moe_gelu, moe_scaled, moe_used, moe_acc, h_moe = [sem(n) for n in (
            "moe_hid", "moe_bc", "moe_gelu", "moe_scaled", "moe_used", "moe_acc", "h_moe")]
        rk_scaled, rk_mm, rk_clip, rk_exp, rk_kv, rk_sums, rk_r, rk_sig, rk_gated, rk_y, h_rwkv = [sem(n) for n in (
            "rk_scaled", "rk_mm", "rk_clip", "rk_exp", "rk_kv", "rk_sums", "rk_r", "rk_sig", "rk_gated", "rk_y", "h_rwkv")]
        s_w2 = sem("late_weights_loaded")
        s_w3 = sem("last_weights_loaded")
        flag_in, flag_all, flag_ready, dve_tail, dve_live, gs_in, gs_out = [sem(n) for n in (
            "flag_in", "flag_all", "flag_ready", "dve_tail", "dve_live", "gs_in", "gs_out")]
        c_loaded, c_keyed, c_gathered, c_diagonal, c_rows, c_chain, c_tabled, c_table_written = [sem(n) for n in (
            "c_loaded", "c_keyed", "c_gathered", "c_diagonal", "c_rows", "c_chain", "c_tabled", "c_table_written")]
        c_free, c_paced, c_finished = sem("c_free"), sem("c_paced"), sem("c_finished")
        c_exp_in, c_exp_out, c_operands, c_summed = [sem(n) for n in ("c_exp_in", "c_exp_out", "c_operands", "c_summed")]
        gathered = [sem("gathered%d" % g) for g in range(GR)]
        gat_mm, hg_ready, hc_loaded, table_written, ge_in, ge_out, f_hid, f_gelu, f_out, f_copied, ones_ready = [sem(n) for n in (
            "gat_mm", "hg_ready", "hc_loaded", "table_written", "ge_in", "ge_out", "f_hid", "f_gelu", "f_out", "f_copied", "ones_ready")]
        outT_mm, outT_copied, s_out = sem("outT_mm"), sem("outT_copied"), sem("s_out")

        block = ctx.enter_context(nc.Block())
        out_v = None if UPTO < 0 else t["out"].rearrange("(h b) l f -> h (b l) f", h=2).rearrange("h (t p) f -> p t h f", p=P)

        def ch(x, c):
            return x[:, c * CH:(c + 1) * CH]

        def seqs(x, k, c, off):
            return x[:, k, 2 * c:2 * c + 2, off:off + L]

        def seq_ps(b):
            return ps[:, b, :].rearrange("p (b l) -> p b l", b=2)

        LN_IN = [(h_tok, lambda c: c + 1), (h_attn, lambda c: 4 * (c + 1)), (h_moe, lambda c: c + 1),
                 (h_rwkv, lambda c: 2 * (c + 1))]

        def normed(k, c):
            return seqs(up, 0, c, 1) if k == 2 else ch(nrm, c)

        def cols2(x, k):
            return x.rearrange("p (b l) -> p b l", b=2) if k == 2 else x

        ON_ACT = [int(e % 5 in (1, 3)) for e in range(QT)]
        N_ACT = sum(ON_ACT)
        N_DVE = QT - N_ACT
        BEFORE = [sum(ON_ACT[:e]) for e in range(QT)]

        def query(e):
            return 8 * (e % 4) + e // 4

        def relu_free(eng, T, e):
            if isinstance(T, int):
                if T * QT + e - NR + 1 > 0:
                    eng.wait_ge(relu_used, T * QT + e - NR + 1)
            else:
                eng.wait_ge(relu_used, T * QT + (e - NR + 1))

        def wait(eng, s, v):
            if not isinstance(v, int) or v > 0:
                eng.wait_ge(s, v)

        e_loaded, e_digits, e_hot, e_hot_used, e_count, e_hsb, e_nd, e_nd_mm = [sem(n) for n in (
            "e_loaded", "e_digits", "e_hot", "e_hot_used", "e_count", "e_hsb", "e_nd", "e_nd_mm")]
        x_hot, x_count, x_cnt, x_off, x_slot, x_slot_used, x_routed, e_iota, e_done = [sem(n) for n in (
            "x_hot", "x_count", "x_cnt", "x_off", "x_slot", "x_slot_used", "x_routed", "e_iota", "e_done")]

        def live_edges_by_column(dve):
            ts, tt, stt = nc.vector.tensor_scalar, nc.vector.tensor_tensor, nc.vector.scalar_tensor_tensor
            att_s = grow[:, 0, :]
            PER = [K_MAX, K_SUM]
            base = [0, GEN * K_MAX + 8]

            def chained(pas, t_):
                n = [0]

                def link(ins):
                    n[0] += 1
                    ins.then_inc(c_chain, 1)
                    dve.wait_ge(c_chain, t_ * PER[pas] + (base[pas] + n[0]))
                return link, n

            def decode(link, pas, t_):
                dve.wait_ge(c_loaded, (t_ + (1 + pas * GEN)) * 32)
                link(ts(c_lo[:, :], c_dst[:, :], P - 1, None, ALU.bitwise_and))
                link(ts(c_q[:, :], c_dst[:, :], 7, None, ALU.logical_shift_right))
                link(ts(c_f[:, 0:1], c_src[:, :], float(M - 1), None, ALU.is_lt))
                link(stt(c_f[:, 0:1], c_q[:, :], float(NQ), c_f[:, 0:1], ALU.is_lt, ALU.mult))
                link(stt(c_f[:, 1:2], c_lo[:, :], 1.0, c_f[:, 0:1], ALU.add, ALU.mult))
                link(ts(c_f[:, 1:2], c_f[:, 1:2], -1.0, None, ALU.add))
                link(nc.vector.tensor_copy(c_f[:, 2:3], c_q[:, :]))
                link(ts(c_di[:, :], c_dst[:, :], float(M - 1), None, ALU.min))
                ts(c_si[:, :], c_src[:, :], float(M - 1), None, ALU.min).then_inc(c_keyed, 1)
                dve.wait_ge(c_keyed, t_ + (1 + pas * GEN))
                nc.vector.memset(c_f[:, 3:4], 0.0).then_inc(c_free, 1)

            def source_scores(link, out_):
                link(tt(c_t[:, :], c_g[:, :], att_s, ALU.mult))
                link(nc.vector.reduce_sum(out_, c_t[:, :].rearrange("p (h e) -> p h e", h=HEADS), AX.X))

            nc.vector.memset(c_f[:, 3:4], 0.0).then_inc(c_free, 1)
            with dve.Fori(0, GEN) as t_:
                link, n = chained(0, t_)
                decode(link, 0, t_)
                dve.wait_ge(c_gathered, (t_ + 1) * 16)
                source_scores(link, c_v[:, 0:4])
                link(nc.vector.tensor_copy(c_v[:, 4:6], c_f[:, 1:3]))
                tt(c_diag, eye[:, :].unsqueeze(1).to_broadcast([P, 6, P]), c_v[:, :].unsqueeze(2).to_broadcast([P, 6, P]),
                   ALU.mult).then_inc(c_diagonal, 1)
                dve.wait_ge(c_rows, t_ + 1)
                link(ts(c_row[:, 0, :], ps[:, 1, P:2 * P], lane_id[:, 0:1], None, ALU.is_equal))
                for q_ in range(NQ):
                    ins = stt(c_mask[:, q_, :], ps[:, 1, 2 * P:3 * P], float(q_), c_row[:, 0, :], ALU.is_equal, ALU.mult)
                link(ins)
                cm = c_mask.rearrange("p q e -> p (q e)")
                link(ts(cm, cm, -1.0, BIG, ALU.add, ALU.mult))
                for hd in range(HEADS):
                    row = ps[:, hd // 3, (hd % 3) * P:(hd % 3 + 1) * P]
                    link(tt(c_pick, c_mask, row.unsqueeze(1).to_broadcast([P, NQ, P]), ALU.add))
                    link(nc.vector.reduce_max(c_top[:, :], c_pick, AX.X))
                    link(tt(a_top[:, :, hd], a_top[:, :, hd], c_top[:, :], ALU.max))
                assert n[0] == K_MAX, n[0]
            n = [GEN * K_MAX]

            def link(ins):
                n[0] += 1
                ins.then_inc(c_chain, 1)
                dve.wait_ge(c_chain, n[0])

            link(tt(a_y, a_top, a_dst, ALU.add))
            link(stt(a_top.rearrange("p q h -> p (q h)"), a_y.rearrange("p q h -> p (q h)"), 0.2,
                     a_y.rearrange("p q h -> p (q h)"), ALU.mult, ALU.max))
            link(nc.vector.memset(num, 0.0))
            link(nc.vector.memset(den, 0.0))
            link(nc.vector.tensor_copy(c_tab[:, :, 0:4], a_dst))
            link(nc.vector.tensor_copy(c_tab[:, :, 4:8], a_top))
            link(nc.vector.memset(c_top[:, :], 0.0))
            link(nc.vector.memset(c_t[:, :], 0.0))
            nc.vector.memset(c_row[:, 1, :], 0.0).then_inc(c_tabled, 1)
            with dve.Fori(0, GEN) as t_:
                link, n = chained(1, t_)
                decode(link, 1, t_)
                dve.wait_ge(c_gathered, t_ * 32 + (GEN * 16 + 32))
                source_scores(link, c_e[:, 0:4])
                e4 = c_e[:, 0:4]
                link(tt(e4, e4, c_d[:, 0:4], ALU.add))
                link(stt(e4, e4, 0.2, e4, ALU.mult, ALU.max))
                link(tt(e4, e4, c_d[:, 4:8], ALU.subtract))
                ts(e4, e4, 0.0, None, ALU.min).then_inc(c_exp_in, 1)
                dve.wait_ge(c_exp_out, t_ + 1)
                link(tt(c_e[:, 4:20].rearrange("p (h e) -> p h e", h=HEADS), c_g[:, :].rearrange("p (h e) -> p h e", h=HEADS),
                        e4.unsqueeze(2).to_broadcast([P, HEADS, 4]), ALU.mult))
                link(ts(c_top[:, :], idxQ[:, :], c_f[:, 2:3], None, ALU.is_equal))
                link(tt(c_rhs, c_top[:, :].unsqueeze(2).to_broadcast([P, NQ, 20]), c_e[:, :].unsqueeze(1).to_broadcast([P, NQ, 20]), ALU.mult))
                ts(c_hot, idx128[:, :], c_f[:, 1:2], None, ALU.is_equal).then_inc(c_operands, 1)
                dve.wait_ge(c_summed, t_ + 1)
                for j in range(2):
                    part = ps[:, j, 0:16 * 20].rearrange("p (q v) -> p q v", q=16)
                    qs = slice(16 * j, 16 * j + 16)
                    link(tt(den[:, qs, :], den[:, qs, :], part[:, :, 0:4], ALU.add))
                    link(tt(num[:, qs, :], num[:, qs, :], part[:, :, 4:20], ALU.add))
                assert n[0] == K_SUM, n[0]
            nc.vector.memset(c_f[:, 3:4], 0.0).then_inc(c_finished, 1)

        def attend_and_mix(dve, link):
            ts, tt, stt = nc.vector.tensor_scalar, nc.vector.tensor_tensor, nc.vector.scalar_tensor_tensor
            att_s, att_d, b_gat, gamma, beta = [grow[:, j, :] for j in range(5)]

            def nodes(x):
                return x.unsqueeze(1).to_broadcast([P, NQ, 16])

            def q4(x):
                return x.rearrange("p q (h e) -> p q h e", h=HEADS)

            def flat(x, s_="p q f -> p (q f)"):
                return x.rearrange(s_)

            for g in range(GR):
                for ql in range(QG):
                    link(ts(pn[:, g, ql, :], q1f[:, g * GS:(g + 1) * GS], float(g * QG + ql + 1), -1.0, ALU.is_equal, ALU.add))
            link(ts(flat(pn, "p g q w -> p (g q w)"), flat(pn, "p g q w -> p (g q w)"), BIG, None, ALU.mult))
            dve.wait_ge(s_w3, 6 * 16)
            dve.wait_ge(gat_mm, 1)
            nc.vector.tensor_copy(hg.rearrange("p (h t) f -> p t h f", h=2),
                                  ps[:, 7, :].rearrange("p (t h f) -> p t h f", t=TILES, h=2)).then_inc(hg_ready, 1)
            dve.wait_ge(hg_ready, 1)
            for a_, o_ in ((att_s, a_self), (att_d, a_dst)):
                link(tt(gtmp, hg, nodes(a_), ALU.mult))
                link(nc.vector.reduce_sum(o_, q4(gtmp), AX.X))
            link(ts(pen, nd[:, :], 0.0, -1.0, ALU.is_gt, ALU.add))
            link(ts(pen, pen, BIG, None, ALU.mult))
            dve.wait_ge(hc_loaded, 16)
            link(tt(hct, hc, att_s, ALU.mult))
            link(nc.vector.reduce_sum(a_c, hct.rearrange("p (h e) -> p h e", h=HEADS), AX.X))
            link(tt(aliased, pen.unsqueeze(2).to_broadcast([P, NQ, HEADS]), a_c.unsqueeze(1).to_broadcast([P, NQ, HEADS]), ALU.add))
            link(tt(a_top, a_self, aliased, ALU.max))
            dve.wait_ge(flag_ready, 1)
            over = dve.value_load(flag_i[0:1, 0:1], min_val=0, max_val=1)
            nl = [0]

            def link_live(ins):
                nl[0] += 1
                ins.then_inc(dve_live, 1)
                dve.wait_ge(dve_live, nl[0])

            with dve.If(over < 1):
                for g in range(GR):
                    G_ = gath[:, g * GS:(g + 1) * GS, :]
                    S_ = g_src[:, g * GS:(g + 1) * GS, :]
                    qs = slice(g * QG, (g + 1) * QG)
                    dve.wait_ge(gathered[g], 16 * GS)
                    link_live(tt(g_tmp, G_, att_s.unsqueeze(1).to_broadcast([P, GS, 16]), ALU.mult))
                    link_live(nc.vector.reduce_sum(S_, g_tmp.rearrange("p w (h e) -> p w h e", h=HEADS), AX.X))
                    link_live(tt(t1, S_.rearrange("p w h -> p h w").unsqueeze(2).to_broadcast([P, HEADS, QG, GS]),
                            pn[:, g, :, :].unsqueeze(1).to_broadcast([P, HEADS, QG, GS]), ALU.add))
                    link_live(nc.vector.reduce_max(g_top, t1, AX.X))
                    top = a_top[:, qs, :].rearrange("p q h -> p h q")
                    link_live(tt(top, top, g_top, ALU.max))
                    link_live(tt(a_y[:, qs, :], a_top[:, qs, :], a_dst[:, qs, :], ALU.add))
                    link_live(stt(a_top[:, qs, :], a_y[:, qs, :], 0.2, a_y[:, qs, :], ALU.mult, ALU.max))

                    def over_w(x):
                        return x[:, qs, :].rearrange("p q h -> p h q").unsqueeze(3).to_broadcast([P, HEADS, QG, GS])

                    link_live(tt(t1, t1, over_w(a_dst), ALU.add))
                    t1f = t1.rearrange("p h q w -> p (h q w)")
                    link_live(stt(t1f, t1f, 0.2, t1f, ALU.mult, ALU.max))
                    tt(t1, t1, over_w(a_top), ALU.subtract).then_inc(ge_in, 1)
                    dve.wait_ge(ge_out, g + 1)
                    link_live(nc.vector.reduce_sum(den[:, qs, :].rearrange("p q h -> p h q"), t1, AX.X))
                    for hd in range(HEADS):
                        link_live(tt(t2, t1[:, hd, :, :].unsqueeze(1).to_broadcast([P, 4, QG, GS]),
                                G_[:, :, 4 * hd:4 * hd + 4].rearrange("p w e -> p e w").unsqueeze(2).to_broadcast([P, 4, QG, GS]), ALU.mult))
                        link_live(nc.vector.reduce_sum(num[:, qs, 4 * hd:4 * hd + 4].rearrange("p q e -> p e q"), t2, AX.X))
            with dve.Else():
                live_edges_by_column(dve)
            nt = [0]

            def link_tail(ins):
                nt[0] += 1
                ins.then_inc(dve_tail, 1)
                dve.wait_ge(dve_tail, nt[0])

            link_tail(tt(e_small[:, 0, :, :], a_self, a_dst, ALU.add))
            link_tail(tt(e_small[:, 1, :, :], aliased, a_dst, ALU.add))
            ef = e_small.rearrange("p a q h -> p (a q h)")
            link_tail(stt(ef, ef, 0.2, ef, ALU.mult, ALU.max))
            link_tail(tt(e_small[:, 0, :, :], e_small[:, 0, :, :], a_top, ALU.subtract))
            tt(e_small[:, 1, :, :], e_small[:, 1, :, :], a_top, ALU.subtract).then_inc(gs_in, 1)
            dve.wait_ge(gs_out, 1)
            link_tail(tt(e_small[:, 1, :, :], e_small[:, 1, :, :], nd[:, :].unsqueeze(2).to_broadcast([P, NQ, HEADS]), ALU.mult))
            for j in range(2):
                e_ = e_small[:, j, :, :]
                link_tail(tt(den, den, e_, ALU.add))
                link_tail(tt(q4(gtmp), e_.unsqueeze(3).to_broadcast([P, NQ, HEADS, 4]), q4(hg) if j == 0 else q4(nodes(hc)), ALU.mult))
                link_tail(tt(num, num, gtmp, ALU.add))
            denf = den.rearrange("p q h -> p (q h)")
            link_tail(ts(denf, denf, 1e-16, None, ALU.add))
            link_tail(nc.vector.reciprocal(denf, denf))
            link_tail(tt(q4(num), q4(num), den.unsqueeze(3).to_broadcast([P, NQ, HEADS, 4]), ALU.mult))
            link_tail(tt(num, num, nodes(b_gat), ALU.add))
            link_tail(nc.vector.reduce_sum(mu, num, AX.X))
            link_tail(ts(mu, mu, 1 / 16, None, ALU.mult))
            link_tail(tt(num, num, mu.unsqueeze(2).to_broadcast([P, NQ, 16]), ALU.subtract))
            link_tail(tt(gtmp, num, num, ALU.mult))
            nc.vector.reduce_sum(mu, gtmp, AX.X).then_inc(gs_in, 1)
            dve.wait_ge(gs_out, 2)
            link_tail(nc.vector.reciprocal(rstd, mu))
            link_tail(tt(num, num, rstd.unsqueeze(2).to_broadcast([P, NQ, 16]), ALU.mult))
            link_tail(tt(num, num, nodes(gamma), ALU.mult))
            link_tail(tt(num, num, nodes(beta), ALU.add))
            link_tail(nc.vector.reduce_sum(tl, num.rearrange("p q (h e) -> p q e h", h=HEADS), AX.X))
            tlf = tl.rearrange("p q e -> p (q e)")
            link_tail(ts(tlf, tlf, 1 / HEADS, None, ALU.mult))

            def over_e1(x):
                return x.unsqueeze(2).to_broadcast([P, NQ, E1])

            ranks1 = rank_w[:, E - E1:E].unsqueeze(1).to_broadcast([P, NQ, E1])
            link_tail(nc.vector.reduce_max(tm1, tl, AX.X))
            tt(t_l2, tl, over_e1(tm1), ALU.subtract).then_inc(gs_in, 1)

            def first1(x, largest, pick_out):
                link_tail(tt(te, x, over_e1(largest), ALU.is_equal))
                link_tail(tt(te, te, ranks1, ALU.mult))
                link_tail(nc.vector.reduce_max(tmr, te, AX.X))
                link_tail(tt(pick_out, te, over_e1(tmr), ALU.is_equal))

            first1(tl, tm1, t_1)
            link_tail(stt(tl, t_1, -BIG, tl, ALU.mult, ALU.add))
            link_tail(nc.vector.reduce_max(tm1, tl, AX.X))
            first1(tl, tm1, t_2)
            link_tail(tt(t_1, t_1, t_2, ALU.add))
            dve.wait_ge(gs_out, 3)
            link_tail(tt(t_1, t_1, t_l2, ALU.mult))
            link_tail(nc.vector.reduce_sum(tm1, t_1, AX.X))
            link_tail(nc.vector.reciprocal(tm1, tm1))
            link_tail(tt(g2.rearrange("p (t h) e -> p t h e", h=2), t_1.rearrange("p (h t) e -> p t h e", h=2),
                    tm1.rearrange("p (h t) -> p t h", h=2).unsqueeze(3).to_broadcast([P, TILES, 2, E1]), ALU.mult))
            dve.wait_ge(f_copied, 32)
            link_tail(tt(yb, yb, g2.rearrange("p q e -> p (q e)").unsqueeze(2).to_broadcast([P, NQ * E1, D]), ALU.mult))
            link_tail(nc.vector.reduce_sum(outY.rearrange("p t h f -> p (t h) f"), yb.rearrange("p (q e) f -> p q f e", e=E1), AX.X))
            for j in range(4):
                dve.wait_ge(outT_mm, 4 * (j + 1))
                o_ = outY[:, 4 * j:4 * j + 4, :, :].rearrange("p t h f -> p (t h f)")
                tt(o_, o_, ps[:, j, :], ALU.add).then_inc(outT_copied, 1)

        def edges_dve(dve, link):
            ts, tt, stt = nc.vector.tensor_scalar, nc.vector.tensor_tensor, nc.vector.scalar_tensor_tensor
            dve.wait_ge(e_loaded, 32)
            ts(e_lo, e_dst, P - 1, None, ALU.bitwise_and)
            ts(e_q, e_dst, 7, None, ALU.logical_shift_right)
            link(ts(e_tmp, e_src, float(M - 1), None, ALU.is_lt))
            link(stt(e_tmp, e_q, float(NQ), e_tmp, ALU.is_lt, ALU.mult))
            link(stt(e_key, e_q, float(M), e_src, ALU.mult, ALU.add))
            link(stt(e_key, e_lo, float(NQ * M), e_key, ALU.mult, ALU.add))
            link(stt(e_key, e_key, 1.0, e_tmp, ALU.add, ALU.mult))
            link(stt(e_tmp, e_q, float(NQ), e_tmp, ALU.is_lt, ALU.subtract))
            ts(e_lo, e_dst, 63, None, ALU.bitwise_and)
            link(ts(e_q, e_dst, 6, None, ALU.logical_shift_right))
            ts(d_hi, e_q, 2048.0, None, ALU.min)
            link(stt(e_tmp, e_lo, 1.0, e_tmp, ALU.add, ALU.mult))
            link(ts(d_lo, e_tmp, -1.0, None, ALU.add))
            dve.wait_ge(e_iota, 6)
            for n in range(EPP // HT):
                if n >= 2:
                    dve.wait_ge(e_hot_used, n - 1)
                for dst, d in ((hot_lo[n % 2], d_lo), (hot_hi[n % 2], d_hi)):
                    ins = tt(dst, d[:, n * HT:(n + 1) * HT].unsqueeze(1).to_broadcast([P, 64, HT]), iota_x, ALU.is_equal)
                ins.then_inc(e_hot, 1)
            dve.wait_ge(e_hot_used, EPP // HT)
            for c in range(2):
                part = e_key[:, c * EPP // 2:(c + 1) * EPP // 2]
                for j in range(XC // 8):
                    k8 = x_key[:, c * XC + 8 * j:c * XC + 8 * j + 8]
                    link(nc.vector.max(k8, part))
                    link(nc.vector.match_replace(part, k8, part, 0.0))
            link(nc.vector.reduce_max(bad[:, 0:1], e_key, AX.X))
            link(ts(x_key, x_key, -1.0, None, ALU.add))
            link(nc.vector.tensor_copy(x_i, x_key))
            ts(x_b, x_i, 17, None, ALU.arith_shift_right)
            link(ts(x_t1, x_i, NQ * M - 1, None, ALU.bitwise_and))
            nc.vector.tensor_copy(x_bf, x_b)
            ts(x_t2, x_t1, 8, None, ALU.logical_shift_right)
            link(ts(x_t1, x_t1, 255, None, ALU.bitwise_and))
            ts(x_A, x_t2, 16.0, None, ALU.add)
            link(nc.vector.tensor_copy(x_B, x_t1))
            for t_ in range(XT):
                ins = ts(hot[:, t_, :], idx128[:, :], x_bf[:, t_:t_ + 1], None, ALU.is_equal)
                if t_ % 16 == 15:
                    ins.then_inc(x_hot, 1)
            link(nc.vector.memset(x_zero, 0.0))
            for c in range(2):
                a, b_ = c * XC, (c + 1) * XC
                link(nc.vector.memset(x_new[:, a:a + 1], 1.0))
                link(tt(x_new[:, a + 1:b_], x_bf[:, a + 1:b_], x_bf[:, a:b_ - 1], ALU.not_equal))
                link(tt(x_new[:, a:b_], x_new[:, a:b_], idxXT[:, a:b_], ALU.mult))
                link(nc.vector.tensor_tensor_scan(x_run[:, a:b_], x_zero[:, a:b_], x_new[:, a:b_], 0.0, ALU.max, ALU.max))
            link(tt(x_rank, idxXT[:, :], x_run, ALU.subtract))
            dve.wait_ge(x_count, 1)
            nc.vector.tensor_copy(cnt_sb, ps[:, 0:2, 0:P]).then_inc(x_cnt, 1)
            dve.wait_ge(x_off, 1)
            nc.vector.tensor_copy(off_sb[:, 0, :], ps[:, 2, 0:P])
            nc.vector.tensor_copy(off_sb[:, 1, :], ps[:, 3, 0:P])
            link(nc.vector.reduce_max(bad[:, 1:2], ps[:, 4, 0:P], AX.X))
            n8 = XT // 8
            for j in range(8):
                a = j * n8
                link(tt(hot_off, hot[:, a:a + n8, :], off_sb[:, j // 4, :].unsqueeze(1).to_broadcast([P, n8, P]), ALU.mult))
                link(nc.vector.reduce_sum(x_new[:, a:a + n8], hot_off, AX.X))
            link(tt(x_rank, x_rank, x_new, ALU.add))
            for t_ in range(XT):
                if t_ >= 4:
                    dve.wait_ge(x_slot_used, t_ - 3)
                for j, x in enumerate((x_A, x_B)):
                    ins = ts(slot_hot[t_ % 4][:, j, :], idxW[:, :], x_rank[:, t_:t_ + 1], x[:, t_:t_ + 1], ALU.is_equal, ALU.mult)
                ins.then_inc(x_slot, 1)
            dve.wait_ge(x_routed, 1)
            link(nc.vector.tensor_copy(l_m, ps[:, 5, WL:2 * WL]))
            link(stt(l_key, ps[:, 5, 0:WL], 256.0, l_m, ALU.mult, ALU.add))
            for g in range(GR):
                lo, hi = M * (1 + g * QG), M * (1 + (g + 1) * QG)
                link(stt(l_m, l_key, float(lo), l_key, ALU.is_ge, ALU.mult))
                link(stt(l_g, l_key, float(hi), l_m, ALU.is_lt, ALU.mult))
                for j in range(GS // 8):
                    k8 = s_key[:, g, 8 * j:8 * j + 8]
                    link(nc.vector.max(k8, l_g))
                    link(nc.vector.match_replace(l_g, k8, l_g, 0.0))
                link(nc.vector.reduce_max(l_m[:, g:g + 1], l_g, AX.X) if False else nc.vector.reduce_max(bad[:, 2:3] if g == 0 else bad[:, 3:4], l_g, AX.X))
                if g >= 2:
                    link(tt(bad[:, 2:3], bad[:, 2:3], bad[:, 3:4], ALU.max))
                elif g == 1:
                    link(tt(bad[:, 2:3], bad[:, 2:3], bad[:, 3:4], ALU.max))
            dve.wait_ge(e_nd_mm, 1)
            link(nc.vector.tensor_copy(nd[:, :], ps[:, 7, 0:NQ]))
            link(ts(flag[:, 0:1], bad[:, 1:2], -float(WL), None, ALU.add))
            link(tt(flag[:, 0:1], flag[:, 0:1], bad[:, 0:1], ALU.max))
            tt(flag[:, 0:1], flag[:, 0:1], bad[:, 2:3], ALU.max).then_inc(flag_in, 1)
            dve.wait_ge(flag_all, 1)
            link(ts(flag[:, 1:2], flag[:, 1:2], 0.0, 1.0, ALU.max, ALU.min))
            nc.vector.tensor_copy(flag_i[:, :], flag[0:1, 1:2]).then_inc(flag_ready, 1)
            flat = s_key[:, :, :].rearrange("p g s -> p (g s)")
            link(nc.vector.tensor_copy(s_idx[:, :], flat))
            link(ts(x_i[:, 0:XT] if False else l_i, s_idx[:, :], 12, None, ALU.logical_shift_right))
            nc.vector.tensor_copy(q1f[:, :], l_i)
            link(ts(s_idx[:, :], s_idx[:, :], M - 1, None, ALU.bitwise_and))

        def edges_pe(pe):
            mm = nc.tensor.matmul
            for n in range(EPP // HT):
                pe.wait_ge(e_hot, n + 1)
                for j in range(HT):
                    ins = mm(ps[0:64, 6, 0:64], hot_lo[n % 2][:, :, j], hot_hi[n % 2][:, :, j],
                             start=(n == 0 and j == 0), stop=(n == EPP // HT - 1 and j == HT - 1))
                ins.then_inc(e_hot_used, 1)
            for t_ in range(XT):
                if t_ % 16 == 0:
                    pe.wait_ge(x_hot, t_ // 16 + 1)
                    if t_ == 0:
                        pe.wait_ge(e_iota, 6)
                ins = mm(ps[:, t_ // XC, 0:P], cst[:, 0, :], hot[:, t_, :], start=(t_ % XC == 0), stop=(t_ % XC == XC - 1))
            ins.then_inc(x_count, 1)
            pe.wait_ge(e_hsb, 1)
            for j in range(2):
                ins = mm(ps[:, 7, 0:NQ], half_f[0:64, j, :], hsb[:, j::2], start=(j == 0), stop=(j == 1))
            ins.then_inc(e_nd_mm, 1)
            pe.wait_ge(x_cnt, 1)
            LOW, ONES = cst[:, 1, :], cst[:, 2, :]
            mm(ps[:, 2, 0:P], LOW, cnt_sb[:, 0, :], start=True, stop=True)
            mm(ps[:, 3, 0:P], ONES, cnt_sb[:, 0, :], start=True, stop=False)
            mm(ps[:, 3, 0:P], LOW, cnt_sb[:, 1, :], start=False, stop=True)
            mm(ps[:, 4, 0:P], ONES, cnt_sb[:, 0, :], start=True, stop=False)
            mm(ps[:, 4, 0:P], ONES, cnt_sb[:, 1, :], start=False, stop=True).then_inc(x_off, 1)
            for t_ in range(XT):
                pe.wait_ge(x_slot, t_ + 1)
                ins = mm(ps[:, 5, 0:2 * WL], hot[:, t_, :], slot_hot[t_ % 4].rearrange("p a b -> p (a b)"),
                         start=(t_ == 0), stop=(t_ == XT - 1))
                ins.then_inc(x_slot_used, 1)
            pe.wait_ge(x_slot_used, XT)
            mm(ps[0:32, 4, 256:257], eye[:, 0:32], eye[:, 0:1], start=True, stop=True).then_inc(x_routed, 1)

        def edges_act(act):
            act.wait_ge(e_hot_used, EPP // HT)
            act.activation(hsb[:, :], ps[0:64, 6, 0:64], ACT.Copy).then_inc(e_hsb, 1)

        def load_column(act, pas, t_):
            act.wait_ge(c_free, t_ + (pas * GEN + 1))
            for dst, k in ((c_src, 0), (c_dst, 1)):
                act.dma_start(dst[:, :], edge_cols[k][:, ds(t_, 1)], allow_slow_non_contiguous=True).then_inc(c_loaded, 16)

        edge_cols = t["edges"].rearrange("a (p k) -> a p k", p=P)

        def gather_live(pool):
            for w_ in range(GR * GS):
                nc.gpsimd.indirect_dma_start(gath[:, w_, :], None, table,
                                                 bass.IndirectOffsetOnAxis(ap=s_idx[:, w_:w_ + 1], axis=0)).then_inc(gathered[w_ // GS], 16)

        @block.gpsimd
        def _(pool):
            nc.gpsimd.iota(idx128[:, :], [[1, P]], base=0, channel_multiplier=0, allow_small_or_imprecise_dtypes=True).then_inc(e_iota, 1)
            nc.gpsimd.iota(idxW[:, :], [[1, WL]], base=0, channel_multiplier=0, allow_small_or_imprecise_dtypes=True).then_inc(e_iota, 1)
            nc.gpsimd.iota(idxXT[:, :], [[1, XT]], base=0, channel_multiplier=0, allow_small_or_imprecise_dtypes=True).then_inc(e_iota, 1)
            nc.gpsimd.iota(iota_x, [[1, 64], [0, HT]], base=0, channel_multiplier=0, allow_small_or_imprecise_dtypes=True).then_inc(e_iota, 1)

            nc.gpsimd.memset(c_w[:, :], 0.0).then_inc(c_paced, 1)
            nc.gpsimd.iota(lane_id[:, :], [[1, 1]], base=0, channel_multiplier=1, allow_small_or_imprecise_dtypes=True).then_inc(e_iota, 1)
            nc.gpsimd.iota(idxQ[:, :], [[1, NQ]], base=0, channel_multiplier=0, allow_small_or_imprecise_dtypes=True).then_inc(e_iota, 1)
            pool.wait_ge(flag_in, 1)
            nc.gpsimd.partition_all_reduce(flag[:, 1:2], flag[:, 0:1], P, bass.bass_isa.ReduceOp.max).then_inc(flag_all, 1)
            if UPTO >= 4:
                pool.wait_ge(e_done, 1)
                pool.wait_ge(flag_ready, 1)
                pool.wait_ge(table_written, 16)
                over = pool.value_load(flag_i[0:1, 0:1], min_val=0, max_val=1)
                with pool.If(over < 1):
                    gather_live(pool)
                with pool.Else():
                    with pool.Fori(0, GEN) as t_:
                        pool.wait_ge(c_paced, t_ + 1)
                        pool.wait_ge(c_keyed, t_ + 1)
                        nc.gpsimd.tensor_tensor(c_w[:, 1:2], c_w[:, 0:1], c_w[:, 0:1], ALU.add).then_inc(c_paced, 1)
                        nc.gpsimd.indirect_dma_start(c_g[:, :], None, table,
                                                     bass.IndirectOffsetOnAxis(ap=c_si[:, 0:1], axis=0)).then_inc(c_gathered, 16)
                    pool.wait_ge(c_table_written, 16)
                    with pool.Fori(0, GEN) as t_:
                        pool.wait_ge(c_paced, t_ + (GEN + 1))
                        pool.wait_ge(c_keyed, t_ + (GEN + 1))
                        nc.gpsimd.tensor_tensor(c_w[:, 1:2], c_w[:, 0:1], c_w[:, 0:1], ALU.add).then_inc(c_paced, 1)
                        nc.gpsimd.indirect_dma_start(c_g[:, :], None, table,
                                                     bass.IndirectOffsetOnAxis(ap=c_si[:, 0:1], axis=0)).then_inc(c_gathered, 16)
                        nc.gpsimd.indirect_dma_start(c_d[:, :], None, table2,
                                                     bass.IndirectOffsetOnAxis(ap=c_di[:, 0:1], axis=0)).then_inc(c_gathered, 16)

        @block.sync
        def _(sp):
            if UPTO < 0 or UPTO >= 4:
                edge = t["edges"].rearrange("a (p k) -> a p k", p=P)
                sp.dma_start(e_src, edge[0]).then_inc(e_loaded, 16)
                sp.dma_start(e_dst, edge[1]).then_inc(e_loaded, 16)
                sp.dma_start(cst[:, :, :].rearrange("p a b -> p (a b)"), t["cst"]).then_inc(s_c, 16)
                sp.dma_start(half_f[:, :, :].rearrange("p a b -> p (a b)"), t["half_f"]).then_inc(s_c, 16)
                sp.dma_start(eye[:, :], t["eye"]).then_inc(s_c, 16)
            if UPTO < 0:
                sp.wait_ge(e_done, 1)
                sp.dma_start(t["out"][:, 0:256], s_key[:, :, :].rearrange("p g s -> p (g s)")).then_inc(s_out, 16)
                sp.dma_start(t["out"][:, 256:288], nd[:, :]).then_inc(s_out, 16)
                sp.dma_start(t["out"][:, 288:292], bad[:, :]).then_inc(s_out, 16)
                sp.wait_ge(s_out, 48)
                return
            if UPTO >= 4:
                sp.wait_ge(e_done, 1)
            sp.dma_start(x_sb[:, :], t["x"]).then_inc(s_x, 16)
            sp.dma_start(wt_sb[:, :], t["wtok"]).then_inc(s_x, 16)
            sp.dma_start(c_sb[:, :], t["cols"]).then_inc(s_w, 16)
            sp.dma_start(w_sb[:, :], t["wmat"]).then_inc(s_w, 16)
            sp.dma_start(slide[:, :], t["slide"]).then_inc(s_w, 16)
            if UPTO < 4:
                sp.dma_start(eye[:, :], t["eye"]).then_inc(s_w, 16)
            for dst, n in ((router[:, :], "router"), (moe_w[:, :, :, :].rearrange("p a e f -> p (a e f)"), "moe_w"),
                           (moe_b2[:, :], "moe_b2"),
                           (pick[:, :, :].rearrange("p e f -> p (e f)"), "pick"), (rank_w[:, :], "rank_w"),
                           (rk_raw[:, :, :].rearrange("p e f -> p (e f)"), "rk"), (wo_sb[:, :], "wo"),
                           (tw[:, :, :].rearrange("p k l -> p (k l)"), "tw"),
                           (tri[:, :, :].rearrange("p k l -> p (k l)"), "tri")):
                sp.dma_start(dst, t[n]).then_inc(s_w2, 16)
            if UPTO >= 4:
                for dst, n in ((w_gat[:, :], "w_gat"), (grow[:, :, :].rearrange("p a f -> p (a f)"), "grow"),
                               (w1s[:, :, :].rearrange("p e f -> p (e f)"), "w1s"),
                               (w2s[:, :, :].rearrange("p e f -> p (e f)"), "w2s"), (f_b1[:, :], "f_b1"),
                               (b2r[:, :, :].rearrange("p e f -> p (e f)"), "b2r")):
                    sp.dma_start(dst, t[n]).then_inc(s_w3, 16)
                sp.wait_ge(hg_ready, 1)
                sp.dma_start(table.rearrange("(q p) f -> p q f", p=P), hg).then_inc(table_written, 16)
                sp.wait_ge(table_written, 16)
                sp.dma_start(hc, table[M - 1:M, :].to_broadcast([P, 16])).then_inc(hc_loaded, 16)
            if UPTO >= 4:
                sp.wait_ge(flag_ready, 1)
                over = sp.value_load(flag_i[0:1, 0:1], min_val=0, max_val=1)
                with sp.If(over < 1):
                    sp.nop()
                with sp.Else():
                    sp.wait_ge(c_tabled, 1)
                    sp.dma_start(table2.rearrange("(q p) f -> p q f", p=P), c_tab[:, :, :]).then_inc(c_table_written, 16)
            final = outY if UPTO >= 4 else outT
            sp.wait_ge(outT_copied, 4)
            for hh in range(2):
                sp.dma_start(out_v[:, :, hh, :], final[:, :, hh, :]).then_inc(s_out, 16)
            sp.wait_ge(s_out, 32)

        @block.vector
        def _(dve):
            n = [0]

            def link(ins):
                n[0] += 1
                ins.then_inc(dve_done, 1)
                dve.wait_ge(dve_done, n[0])

            if UPTO < 0 or UPTO >= 4:
                edges_dve(dve, link)
                nc.vector.memset(dyn[:, 4:5], 0.0).then_inc(e_done, 1)
            if UPTO < 0:
                return
            for x in (up, dn):
                for k in range(2):
                    nc.vector.memset(x[:, k, :, 0:1], 0.0)
                    nc.vector.memset(x[:, k, :, L + 1:L + 2], 0.0)
            nc.vector.memset(dyn[:, 3:4], EPS)
            nc.vector.memset(ones_sq[:, :], 1.0)
            nc.vector.memset(ones1[:, :], 1.0).then_inc(ones_ready, 1)
            dve.wait_ge(s_w, 48 if UPTO >= 4 else 64)
            nc.vector.tensor_tensor(dyn[:, 0:1], C["b1"], C["b2"], ALU.add)
            nc.vector.scalar_tensor_tensor(dyn[:, 1:2], C["b4"], 2.0, C["b3"], ALU.mult, ALU.add).then_inc(bias_ready, 1)
            dve.wait_ge(bias_ready, 1)
            for c in range(NCH):
                dve.wait_ge(tok_a, c + 1)
                nc.vector.tensor_scalar(ch(a_sb, c), ps[:, c, :], dyn[:, 0:1], None, ALU.add).then_inc(tok_sum, 1)
            dve.wait_ge(tok_sum, NCH)
            for s in range(1, STEPS):
                for c in range(NCH):
                    for d in range(2):
                        dve.wait_ge(tok_mm, (s - 1) * 8 + 2 * c + d + 1)
                        b = ps[:, 2 * c + d, :]
                        nc.vector.tensor_tensor(b, b, ch(a_sb, c), ALU.add).then_inc(tok_sum, 1)

            def layernorm(k):
                for c in range(NCH):
                    dve.wait_ge(ln_mean, NCH * k + c + 1)
                    nc.vector.tensor_tensor(ch(dev, c), ch(h, c), ps[:, c, :], ALU.subtract).then_inc(ln_dev, 1)
                for c in range(NCH):
                    dve.wait_ge(ln_std, NCH * k + c + 1)
                    link(nc.vector.reciprocal(ch(sq, c), ch(sq, c)))
                    nc.vector.tensor_tensor(normed(k, c), cols2(ch(dev, c), k), cols2(ch(sq, c), k), ALU.mult).then_inc(ln_out, 1)

            if UPTO >= 1:
                layernorm(0)
                for j in range(4):
                    dve.wait_ge(v_mm, j + 1)
                    nc.vector.tensor_copy(v_sb[:, 4 * j:4 * j + 4, :],
                                          ps[:, 4 + j, :].rearrange("p (t f) -> p t f", t=4)).then_inc(v_copied, 1)
                dve.wait_ge(qk_copied, 16)

                def softmax_max(T, par):
                    dve.wait_ge(relu_used, T * QT + QT)
                    nc.vector.tensor_scalar(sc[:, par, :], ps[:, par, 0:L], C["b_mlp"], 0.0,
                                            ALU.add, ALU.max).then_inc(score_read, 1)
                    dve.wait_ge(score_read, T + 1)
                    nc.vector.reduce_max(st[:, par, 0:1], sc[:, par, :], AX.X, negate=True).then_inc(max_ready, 1)

                def softmax_scale(T, par):
                    dve.wait_ge(exp_ready, T + 1)
                    nc.vector.reciprocal(st[:, par, 2:3], st[:, par, 1:2]).then_inc(recip_done, 1)
                    dve.wait_ge(recip_done, T + 1)
                    nc.vector.tensor_scalar(sc[:, par, :], sc[:, par, :], st[:, par, 2:3], None,
                                            ALU.mult).then_inc(prob_ready, 1)

                def add_out(u):
                    dve.wait_ge(ao_T, u + 1)
                    hs = h[:, ds(u * P, P)]
                    nc.vector.tensor_tensor(hs, hs, ps[:, 5, 0:P], ALU.add).then_inc(h_attn, 1)

                def pair_of_batches(pair, first):
                    for k in range(TPP):
                        T = pair * TPP + k
                        last = not (first and k == 0)
                        for e in range(QT):
                            if not ON_ACT[e]:
                                relu_free(dve, T, e)
                                nc.vector.tensor_scalar(relu[:, e % NR, :], nk_sb[:, ds(pair * L, L)],
                                                        nq_sb[:, ds(pair * L + (k * QT + query(e)), 1)], 0.0,
                                                        ALU.subtract, ALU.max).then_inc(relu_dve, 1)
                            if e == 10 and last:
                                softmax_max(T - 1, (k + 1) % 2)
                            if e == 24 and last:
                                softmax_scale(T - 1, (k + 1) % 2)
                            if e == 6 and k % 4 == 3 and not (first and k == 3):
                                add_out(pair * 2 + (k // 4 - 1))

                pair_of_batches(0, True)
                with dve.Fori(1, NB) as pair:
                    pair_of_batches(pair, False)
                softmax_max(NB * TPP - 1, 1)
                softmax_scale(NB * TPP - 1, 1)
                add_out(TILES - 1)

            if UPTO >= 2:
                layernorm(1)
                dve.wait_ge(s_w2, 9 * 16)
                NT = 2 * TILES

                def over_e(x):
                    return x[:, :].unsqueeze(2).to_broadcast([P, NT, E])

                ranks = rank_w[:, :].unsqueeze(1).to_broadcast([P, NT, E])
                dve.wait_ge(lg_mm, 1)
                link(nc.vector.tensor_copy(lg[:, :, :].rearrange("p t e -> p (t e)"), ps[:, 7, 0:NT * E]))
                link(nc.vector.reduce_max(m1[:, :], lg[:, :, :], AX.X))
                nc.vector.tensor_tensor(l2[:, :, :], lg[:, :, :], over_e(m1), ALU.subtract).then_inc(ex_in, 1)

                def first_of_the_largest(x, largest, pick_out):
                    link(nc.vector.tensor_tensor(eq[:, :, :], x[:, :, :], over_e(largest), ALU.is_equal))
                    link(nc.vector.tensor_tensor(eq[:, :, :], eq[:, :, :], ranks, ALU.mult))
                    link(nc.vector.reduce_max(mr[:, :], eq[:, :, :], AX.X))
                    link(nc.vector.tensor_tensor(pick_out[:, :, :], eq[:, :, :], over_e(mr), ALU.is_equal))

                first_of_the_largest(lg, m1, s1)
                link(nc.vector.scalar_tensor_tensor(lg[:, :, :], s1[:, :, :], -BIG, lg[:, :, :], ALU.mult, ALU.add))
                link(nc.vector.reduce_max(m1[:, :], lg[:, :, :], AX.X))
                first_of_the_largest(lg, m1, s2)
                link(nc.vector.tensor_tensor(s1[:, :, :], s1[:, :, :], s2[:, :, :], ALU.add))
                dve.wait_ge(ex_done, 1)
                link(nc.vector.tensor_tensor(s1[:, :, :], s1[:, :, :], l2[:, :, :], ALU.mult))
                link(nc.vector.reduce_sum(m1[:, :], s1[:, :, :], AX.X))
                link(nc.vector.reciprocal(m1[:, :], m1[:, :]))
                nc.vector.tensor_tensor(s1[:, :, :], s1[:, :, :], over_e(m1), ALU.mult).then_inc(cmb_ready, 1)
                for c in range(NCH):
                    dve.wait_ge(cmb_T, c + 1)
                    nc.vector.tensor_copy(ch(cmbF, c), ps[0:16, c, :]).then_inc(cmb_copied, 1)
                for c in range(NCH):
                    for e in range(E):
                        m = c * E + e
                        dve.wait_ge(moe_gelu, m + 1)
                        dve.wait_ge(moe_bc, m + 1)
                        wait(dve, moe_used, m - 1)
                        nc.vector.tensor_tensor(gs[:, m % 2, :], gbuf[:, m % 2, :], ps[:, 2 + m % 2, :],
                                                ALU.mult).then_inc(moe_scaled, 1)
                    link(nc.vector.tensor_tensor(ch(h, c), ch(h, c), ch(nrm, c), ALU.add))
                    dve.wait_ge(moe_acc, c + 1)
                    nc.vector.tensor_tensor(ch(h, c), ch(h, c), ps[:, 4 + c % 2, :], ALU.add).then_inc(h_moe, 1)

            if UPTO >= 3:
                link(nc.vector.tensor_scalar(omix[:, :], c_sb[:, 5:8], -1.0, 1.0, ALU.mult, ALU.add))
                for j in range(3):
                    nc.vector.tensor_scalar(rk_w[:, 0, j, :], rk_raw[:, j, :], c_sb[:, 5 + j:6 + j], None, ALU.mult)
                    ins = nc.vector.tensor_scalar(rk_w[:, 1, j, :], rk_raw[:, j, :], omix[:, j:j + 1], None, ALU.mult)
                ins.then_inc(rk_scaled, 1)
                layernorm(2)

                def time_values(b):
                    bank = ps[:, b % 4, :].rearrange("p (k w f) -> p k w f", k=2, w=2)
                    dve.wait_ge(rk_mm, b + 1)
                    wait(dve, rk_sums, b - 1)
                    nc.vector.tensor_scalar(kT[:, b % 2, :, :], bank[:, :, 0, :], -60.0, 30.0,
                                            ALU.max, ALU.min).then_inc(rk_clip, 1)
                    dve.wait_ge(rk_exp, b + 1)
                    nc.vector.tensor_tensor(kvT[:, b % 2, :, :], kT[:, b % 2, :, :], bank[:, :, 1, :],
                                            ALU.mult).then_inc(rk_kv, 1)

                def gate(b):
                    dve.wait_ge(rk_sums, b + 1)
                    dve.wait_ge(rk_sig, b // 2 + 1)
                    wait(dve, rk_y, b - 1)
                    link(nc.vector.reciprocal(rw[:, b % 2, 0, :], ps[:, 4 + b % 2, 0:L]))
                    link(nc.vector.tensor_tensor(rw[:, b % 2, 0, :], rw[:, b % 2, 0, :], ps[:, 4 + b % 2, L:2 * L], ALU.mult))
                    nc.vector.tensor_tensor(rw[:, b % 2, 1, :], rw[:, b % 2, 0, :], sig[:, b * L:(b + 1) * L],
                                            ALU.mult).then_inc(rk_gated, 1)

                def add_y(b):
                    dve.wait_ge(rk_y, b + 1)
                    hs = h[:, b * L:(b + 1) * L]
                    nc.vector.tensor_tensor(hs, hs, ps[:, 7, 0:L], ALU.add).then_inc(h_rwkv, 1)

                for b in range(NB + 2):
                    if b < NB:
                        time_values(b)
                    if 1 <= b <= NB:
                        gate(b - 1)
                    if b >= 2:
                        add_y(b - 2)

            if UPTO >= 4:
                layernorm(3)
                attend_and_mix(dve, link)
                return


            for j in range(4):
                dve.wait_ge(outT_mm, 4 * (j + 1))
                nc.vector.tensor_copy(outT[:, 4 * j:4 * j + 4, :, :].rearrange("p t h f -> p (t h f)"),
                                      ps[:, j, :]).then_inc(outT_copied, 1)

        def copy_y(act, n):
            hh, c, e = n // (NCH * E1), n // E1 % NCH, n % E1
            act.wait_ge(f_out, n + 1)
            y = yb.rearrange("p (t h e) f -> p t h e f", h=2, e=E1)[:, 4 * c:4 * c + 4, hh, e, :]
            act.activation(y, ps[:, 2 + n % 2, 0:4 * D].rearrange("p (t f) -> p t f", t=4), ACT.Copy).then_inc(f_copied, 1)

        @block.scalar
        def _(act):
            if UPTO < 0 or UPTO >= 4:
                edges_act(act)
            if UPTO < 0:
                return
            act.wait_ge(bias_ready, 1)
            for c in range(NCH):
                act.wait_ge(tok_sum, c + 1)
                for x in (up, dn):
                    act.activation(seqs(x, 0, c, 1), ch(a_sb, c).rearrange("p (b l) -> p b l", b=2),
                                   ACT.Relu).then_inc(tok_relu, 1)
            for s in range(1, STEPS):
                for c in range(NCH):
                    for d, x in enumerate((up, dn)):
                        act.wait_ge(tok_sum, NCH + (s - 1) * 8 + 2 * c + d + 1)
                        act.activation(seqs(x, s % 2, c, 1), seq_ps(2 * c + d), ACT.Relu).then_inc(tok_relu, 1)
            for c in range(NCH):
                act.wait_ge(tok_out_mm, c + 1)
                act.activation(ch(h, c), ps[:, c, :], ACT.Relu, bias=dyn[:, 1:2]).then_inc(h_tok, 1)

            def layernorm(k):
                for c in range(NCH):
                    act.wait_ge(ln_dev, NCH * k + c + 1)
                    act.activation(ch(sq, c), ch(dev, c), ACT.Square).then_inc(ln_sq, 1)
                for c in range(NCH):
                    act.wait_ge(ln_var, NCH * k + c + 1)
                    act.activation(ch(sq, c), ps[:, 4 + c, :], ACT.Sqrt, bias=dyn[:, 3:4]).then_inc(ln_std, 1)

            if UPTO >= 1:
                layernorm(0)
                for c in range(NCH):
                    for d, (x, nx) in enumerate(((q_sb, nq_sb), (k_sb, nk_sb))):
                        act.wait_ge(qk_mm, 2 * c + d + 1)
                        act.activation(ch(x, c), ps[:, (2 * c + d) % 4, :], ACT.Copy).then_inc(qk_copied, 1)
                        act.activation(ch(nx, c), ps[:, (2 * c + d) % 4, :], ACT.Copy, scale=-1.0).then_inc(qk_copied, 1)
                act.wait_ge(qk_copied, 16)
                act.wait_ge(v_copied, 4)

                def softmax_exp(T, par):
                    act.wait_ge(max_ready, T + 1)
                    act.activation(sc[:, par, :], sc[:, par, :], ACT.Exp, bias=st[:, par, 0:1],
                                   accum_out=st[:, par, 1:2]).then_inc(exp_ready, 1)

                def copy_pT(T, par):
                    act.wait_ge(prob_T, T + 1)
                    act.activation(pT[:, par, :, :].rearrange("p k j -> p (k j)"), ps[:, 4, 0:2 * P],
                                   ACT.Copy).then_inc(pT_copied, 1)

                def copy_ao(u):
                    act.wait_ge(pv_mm, 4 * u + 4)
                    act.activation(ao[:, :], ps[:, 6, 0:P], ACT.Copy).then_inc(ao_copied, 1)

                def pair_of_batches(pair, first):
                    for k in range(TPP):
                        T = pair * TPP + k
                        for e in range(QT):
                            if ON_ACT[e]:
                                relu_free(act, T, e)
                                act.activation(relu[:, e % NR, :], k_sb[:, ds(pair * L, L)], ACT.Relu,
                                               bias=q_sb[:, ds(pair * L + (k * QT + query(e)), 1)],
                                               scale=-1.0).then_inc(relu_act, 1)
                            if e == 4 and not (first and k < 2):
                                copy_pT(T - 2, k % 2)
                            if e == 12 and k % 4 == 2 and not (first and k == 2):
                                copy_ao(pair * 2 + (k // 4 - 1))
                            if e == 14 and k == 2:
                                wait(act, pv_mm, pair * TPP)
                                act.activation(vp[:, :, :], v_sb[:, ds(pair * 2, 2), :], ACT.Copy).then_inc(vp_ready, 1)
                            if e == 16 and not (first and k == 0):
                                softmax_exp(T - 1, (k + 1) % 2)

                pair_of_batches(0, True)
                with act.Fori(1, NB) as pair:
                    pair_of_batches(pair, False)
                T = NB * TPP
                copy_pT(T - 2, 0)
                softmax_exp(T - 1, 1)
                copy_pT(T - 1, 1)
                copy_ao(TILES - 1)

            if UPTO >= 2:
                layernorm(1)
                act.wait_ge(ex_in, 1)
                act.activation(l2[:, :, :], l2[:, :, :], ACT.Exp).then_inc(ex_done, 1)
                for m in range(NCH * E):
                    act.wait_ge(moe_hid, m + 1)
                    wait(act, moe_scaled, m - 1)
                    act.activation(gbuf[:, m % 2, :], ps[:, m % 2, :], ACT.Gelu,
                                   bias=C["moe_b1_%d" % (m % E)]).then_inc(moe_gelu, 1)

            if UPTO >= 3:
                layernorm(2)
                for c in range(NCH):
                    act.wait_ge(rk_r, c + 1)
                    act.activation(ch(sig, c), ps[:, 6, :], ACT.Sigmoid).then_inc(rk_sig, 1)
                for b in range(NB):
                    act.wait_ge(rk_clip, b + 1)
                    act.activation(kT[:, b % 2, :, :], kT[:, b % 2, :, :], ACT.Exp).then_inc(rk_exp, 1)

            if UPTO >= 4:
                layernorm(3)
                act.wait_ge(s_w3, 6 * 16)
                for n in range(2 * NCH * E1):
                    hh, c, e = n // (NCH * E1), n // E1 % NCH, n % E1
                    act.wait_ge(f_hid, n + 1)
                    wait(act, f_out, n - 1)
                    act.activation(g1[:, n % 2, :], ps[:, n % 2, :], ACT.Gelu, bias=f_b1[:, e:e + 1]).then_inc(f_gelu, 1)
                    if n:
                        copy_y(act, n - 1)
                copy_y(act, 2 * NCH * E1 - 1)
                act.wait_ge(flag_ready, 1)
                over = act.value_load(flag_i[0:1, 0:1], min_val=0, max_val=1)
                with act.If(over < 1):
                    for g in range(GR):
                        act.wait_ge(ge_in, g + 1)
                        act.activation(t1, t1, ACT.Exp).then_inc(ge_out, 1)
                with act.Else():
                    with act.Fori(0, GEN) as t_:
                        load_column(act, 0, t_)
                    with act.Fori(0, GEN) as t_:
                        load_column(act, 1, t_)
                        act.wait_ge(c_exp_in, t_ + 1)
                        act.activation(c_e[:, 0:4], c_e[:, 0:4], ACT.Exp).then_inc(c_exp_out, 1)
                act.wait_ge(gs_in, 1)
                act.activation(e_small, e_small, ACT.Exp).then_inc(gs_out, 1)
                act.wait_ge(gs_in, 2)
                act.activation(mu, mu, ACT.Sqrt, bias=dyn[:, 3:4], scale=1 / 16).then_inc(gs_out, 1)
                act.wait_ge(gs_in, 3)
                act.activation(t_l2, t_l2, ACT.Exp).then_inc(gs_out, 1)

        @block.tensor
        def _(pe):
            mm = nc.tensor.matmul
            if UPTO < 0 or UPTO >= 4:
                pe.wait_ge(s_c, 48)
                edges_pe(pe)
            if UPTO < 0:
                return
            pe.wait_ge(s_x, 32)
            for c in range(NCH):
                mm(ps[:, c, :], wt_sb[:, 0:P], ch(x_sb, c), start=True, stop=True).then_inc(tok_a, 1)
            pe.wait_ge(s_w, 48 if UPTO >= 4 else 64)
            for s in range(1, STEPS):
                for c in range(NCH):
                    for d, x in enumerate((up, dn)):
                        pe.wait_ge(tok_relu, (s - 1) * 8 + 2 * c + d + 1)
                        if s == 1 and d == 0:
                            pe.wait_ge(tok_sum, min(2 * c + 2, NCH))
                            pe.wait_ge(tok_relu, min(2 * (2 * c + 2), 8))
                        mm(ps[:, 2 * c + d, :].rearrange("p (b l) -> p b l", b=2), W["tok2"],
                           seqs(x, (s - 1) % 2, c, 2 * d), start=True, stop=True).then_inc(tok_mm, 1)
            pe.wait_ge(tok_relu, STEPS * 8)
            for c in range(NCH):
                o = ps[:, c, :].rearrange("p (b l) -> p b l", b=2)
                mm(ps[:, c, :], wt_sb[:, P:2 * P], ch(x_sb, c), start=True, stop=False)
                mm(o, W["tok4"], seqs(up, (STEPS - 1) % 2, c, 0), start=False, stop=False)
                mm(o, W["tok4"], seqs(dn, (STEPS - 1) % 2, c, 2), start=False, stop=True).then_inc(tok_out_mm, 1)

            def layernorm(k):
                for c in range(NCH):
                    pe.wait_ge(LN_IN[k][0], LN_IN[k][1](c))
                    mm(ps[:, c, :], W["mean"], ch(h, c), start=True, stop=True).then_inc(ln_mean, 1)
                for c in range(NCH):
                    pe.wait_ge(ln_sq, NCH * k + c + 1)
                    mm(ps[:, 4 + c, :], W["mean"], ch(sq, c), start=True, stop=True).then_inc(ln_var, 1)

            if UPTO >= 1:
                layernorm(0)
                pe.wait_ge(ln_std, NCH)
                for c in range(NCH):
                    pe.wait_ge(ln_out, c + 1)
                    for d, w in enumerate(("q", "k")):
                        n = 2 * c + d
                        if n >= 4:
                            pe.wait_ge(qk_copied, 2 * (n - 4) + 2)
                        mm(ps[:, n % 4, :], W[w], ch(nrm, c), start=True, stop=True).then_inc(qk_mm, 1)
                for j in range(4):
                    for i in range(4):
                        ins = mm(ps[:, 4 + j, i * P:(i + 1) * P], nrm[:, (4 * j + i) * P:(4 * j + i + 1) * P], W["v"],
                                 start=True, stop=True)
                    ins.then_inc(v_mm, 1)
                pe.wait_ge(qk_copied, 16)
                pe.wait_ge(v_copied, 4)

                def scores(T, pair, k):
                    wait(pe, score_read, T - 1)
                    nd, na = 0, 0
                    for e in range(QT):
                        if ON_ACT[e]:
                            na += 1
                            pe.wait_ge(relu_act, T * N_ACT + na)
                        else:
                            nd += 1
                            pe.wait_ge(relu_dve, T * N_DVE + nd)
                        j, r = e % 4, e // 4
                        ins = mm(ps[32 * j:32 * j + 32, k % 2, 0:L], slide[:, 28 - 4 * r:60 - 4 * r],
                                 relu[:, e % NR, :], start=(r == 0), stop=(r == 7))
                        ins.then_inc(relu_used, 1)

                def transposes(T, par):
                    wait(pe, prob_ready, T + 1)
                    wait(pe, pT_copied, T)
                    for kb in range(2):
                        ins = nc.tensor.transpose(ps[:, 4, kb * P:(kb + 1) * P], sc[:, par, kb * P:(kb + 1) * P], eye[:, :])
                    ins.then_inc(prob_T, 1)

                def values(T, pair, k):
                    pe.wait_ge(pT_copied, T + 1)
                    if k == 0:
                        pe.wait_ge(vp_ready, pair + 1)
                    if k % 4 == 0:
                        wait(pe, ao_copied, T // 4 if isinstance(T, int) else pair * 2 + k // 4)
                    s = k % 4
                    for g in range(NG):
                        lo = (g // G) * D + g % G
                        for kb in range(2):
                            ins = mm(ps[32 * s:32 * s + 32, 6, lo:lo + D - 1:2], pT[:, k % 2, kb, g:P:NG],
                                     vp[:, kb, lo:lo + D - 1:2],
                                     start=(kb == 0), stop=(kb == 1))
                    ins.then_inc(pv_mm, 1)

                def out_T(u):
                    pe.wait_ge(ao_copied, u + 1)
                    wait(pe, h_attn, u)
                    nc.tensor.transpose(ps[:, 5, 0:P], ao[:, :], eye[:, :]).then_inc(ao_T, 1)

                def pair_of_batches(pair, first):
                    for k in range(TPP):
                        T = pair * TPP + k
                        scores(T, pair, k)
                        if not (first and k == 0):
                            transposes(T - 1, (k + 1) % 2)
                        if not (first and k < 2):
                            values(T - 2, pair if k >= 2 else pair - 1, (k - 2) % TPP)
                        if k % 4 == 2 and not (first and k == 2):
                            out_T(pair * 2 + (k // 4 - 1))

                pair_of_batches(0, True)
                with pe.Fori(1, NB) as pair:
                    pair_of_batches(pair, False)
                T = NB * TPP
                transposes(T - 1, 1)
                values(T - 2, NB - 1, TPP - 2)
                values(T - 1, NB - 1, TPP - 1)
                out_T(TILES - 1)

            if UPTO >= 2:
                layernorm(1)
                pe.wait_ge(s_w2, 9 * 16)
                pe.wait_ge(ln_std, NCH * 2)
                pe.wait_ge(ln_out, NCH * 2)
                for i in range(TILES):
                    ins = mm(ps[:, 7, i * 16:(i + 1) * 16], nrm[:, i * P:(i + 1) * P], router[:, :], start=True, stop=True)
                ins.then_inc(lg_mm, 1)
                pe.wait_ge(cmb_ready, 1)
                for i in range(TILES):
                    ins = nc.tensor.transpose(ps[0:16, i // 4, (i % 4) * P:(i % 4 + 1) * P],
                                              s1[:, 2 * i:2 * i + 2, :].rearrange("p h e -> p (h e)"), eye[:, :])
                    if i % 4 == 3:
                        ins.then_inc(cmb_T, 1)

                def expert_out(m):
                    c, e = m // E, m % E
                    pe.wait_ge(moe_scaled, m + 1)
                    if e == 0:
                        wait(pe, h_moe, c - 1)
                    mm(ps[:, 4 + c % 2, :], moe_w[:, 1, e, :], gs[:, m % 2, :], start=(e == 0), stop=False).then_inc(moe_used, 1)
                    if e == E - 1:
                        mm(ps[:, 4 + c % 2, :], moe_b2[:, :], ch(cmbF, c), start=False, stop=True).then_inc(moe_acc, 1)

                pe.wait_ge(cmb_copied, NCH)
                for m in range(NCH * E):
                    c, e = m // E, m % E
                    wait(pe, moe_gelu, m - 1)
                    mm(ps[:, m % 2, :], moe_w[:, 0, e, :], ch(nrm, c), start=True, stop=True).then_inc(moe_hid, 1)
                    wait(pe, moe_scaled, m - 1)
                    mm(ps[:, 2 + m % 2, :], pick[:, e, :], ch(cmbF, c), start=True, stop=True).then_inc(moe_bc, 1)
                    if m:
                        expert_out(m - 1)
                expert_out(NCH * E - 1)

            if UPTO >= 3:
                layernorm(2)
                pe.wait_ge(ln_std, NCH * 3)
                pe.wait_ge(ln_out, NCH * 3)
                pe.wait_ge(rk_scaled, 1)

                def keys_values(b):
                    wait(pe, rk_kv, b - 3)
                    for kb in range(2):
                        for prev in range(2):
                            o = 1 - prev + kb * P
                            ins = mm(ps[:, b % 4, kb * 2 * P:(kb + 1) * 2 * P], up[:, 0, b, o:o + P],
                                     rk_w[:, prev, 0:2, :].rearrange("p w f -> p (w f)"), start=(prev == 0), stop=(prev == 1))
                    ins.then_inc(rk_mm, 1)

                def receptance(c):
                    wait(pe, rk_sig, c)
                    for prev in range(2):
                        ins = mm(seq_ps(6), rk_w[:, prev, 2, :], seqs(up, 0, c, 1 - prev), start=(prev == 0), stop=(prev == 1))
                    ins.then_inc(rk_r, 1)

                def sums(b):
                    pe.wait_ge(rk_kv, b + 1)
                    wait(pe, rk_gated, b - 1)
                    for j, (x, w) in enumerate(((kT, tri), (kvT, tw))):
                        for kb in range(2):
                            ins = mm(ps[:, 4 + b % 2, j * L:(j + 1) * L], x[:, b % 2, kb, :], w[:, kb, :],
                                     start=(kb == 0), stop=(kb == 1))
                    ins.then_inc(rk_sums, 1)

                def project(b):
                    pe.wait_ge(rk_gated, b + 1)
                    wait(pe, h_rwkv, b)
                    mm(ps[:, 7, 0:L], wo_sb[:, :], rw[:, b % 2, 1, :], start=True, stop=True).then_inc(rk_y, 1)

                for c in range(NCH):
                    receptance(c)
                for b in range(NB + 2):
                    if b < NB:
                        keys_values(b)
                    if 1 <= b <= NB:
                        sums(b - 1)
                    if b >= 2:
                        project(b - 2)

            if UPTO >= 4:
                layernorm(3)
                pe.wait_ge(ln_std, NCH * 4)
                pe.wait_ge(ln_out, NCH * 4)
                pe.wait_ge(s_w3, 6 * 16)
                pe.wait_ge(ones_ready, 1)
                for i in range(TILES):
                    ins = mm(ps[:, 7, i * 32:(i + 1) * 32], nrm[:, i * P:(i + 1) * P], w_gat[:, :], start=True, stop=True)
                ins.then_inc(gat_mm, 1)

                def expert(n):
                    e = n % E1
                    pe.wait_ge(f_gelu, n + 1)
                    wait(pe, f_copied, n - 1)
                    for j in range(4):
                        o_ = ps[:, 2 + n % 2, j * D:(j + 1) * D]
                        mm(o_, g1[:, n % 2, j * P:(j + 1) * P], w2s[:, e, :], start=True, stop=False)
                        ins = mm(o_, ones1[:, :], b2r[:, e, :], start=False, stop=True)
                    ins.then_inc(f_out, 1)

                for n in range(2 * NCH * E1):
                    hh, c, e = n // (NCH * E1), n // E1 % NCH, n % E1
                    wait(pe, f_gelu, n - 1)
                    half = slice(hh * D, hh * D + D)
                    mm(ps[:, n % 2, :], w1s[half, e, :], nrm[half, c * CH:(c + 1) * CH], start=True, stop=True).then_inc(f_hid, 1)
                    if n:
                        expert(n - 1)
                expert(2 * NCH * E1 - 1)
                pe.wait_ge(f_copied, 2 * NCH * E1)
                pe.wait_ge(flag_ready, 1)
                over = pe.value_load(flag_i[0:1, 0:1], min_val=0, max_val=1)
                with pe.If(over < 1):
                    pe.nop()
                with pe.Else():
                    with pe.Fori(0, GEN) as t_:
                        pe.wait_ge(c_diagonal, t_ + 1)
                        for j in range(2):
                            ins = mm(ps[:, j, 0:3 * P], ones_sq[:, :], c_diag[:, 3 * j:3 * j + 3, :].rearrange("p r e -> p (r e)"),
                                     start=True, stop=True)
                        ins.then_inc(c_rows, 1)
                    with pe.Fori(0, GEN) as t_:
                        pe.wait_ge(c_operands, t_ + 1)
                        for j in range(2):
                            ins = mm(ps[:, j, 0:16 * 20], c_hot, c_rhs[:, 16 * j:16 * j + 16, :].rearrange("p q v -> p (q v)"),
                                     start=True, stop=True)
                        ins.then_inc(c_summed, 1)
                    pe.wait_ge(c_finished, 1)

            last, need = {4: (h_rwkv, NB), 0: (h_tok, NCH), 1: (h_attn, TILES), 2: (h_moe, NCH), 3: (h_rwkv, NB)}[UPTO]
            pe.wait_ge(last, need)
            for i in range(TILES):
                nc.tensor.transpose(ps[:, i // 4, (i % 4) * P:(i % 4 + 1) * P], h[:, i * P:(i + 1) * P],
                                    eye[:, :]).then_inc(outT_mm, 1)


_OUTS = [((16, 256, 64), "float32")] if UPTO >= 0 else [((128, 292), "float32")]


def kernel(**inputs):
    import numpy as np
    import concourse.bacc as _bacc
    from concourse import mybir as _mybir
    from concourse.bass_utils import run_bass_kernel_spmd as _run

    i = {k: np.ascontiguousarray(v) for k, v in inputs.items()}
    f32 = np.float32

    def diag(w):
        a, b = w.shape
        o = np.zeros((2 * a, 2 * b), f32)
        o[:a, :b] = w
        o[a:, b:] = w
        return o

    def twice(v):
        return np.concatenate([v, v]).reshape(128, 1)

    arrays = {}
    arrays["x"] = np.ascontiguousarray(i["x"].reshape(2, 8, 4, 256).transpose(0, 2, 1, 3).reshape(8, 2048))
    arrays["wtok"] = np.concatenate([diag(i["L0_tok_W1"].T), diag(i["L0_tok_W3"].T)], 1)
    mean = diag(np.full((64, 64), 1 / 64, f32))
    arrays["wmat"] = np.concatenate([
        diag(i["L0_tok_W2"].T), diag(i["L0_tok_W4"].T), diag(i["L0_attn_Wq"].T), diag(i["L0_attn_Wk"].T),
        diag(i["L0_attn_Wv"].T), mean], 1)
    arrays["cols"] = np.concatenate([twice(i["L0_tok_b%d" % k]) for k in (1, 2, 3, 4)]
                                    + [np.full((128, 1), i["L0_attn_b_mlp"][0], f32)]
                                    + [twice(i["L1_attn_time_mix_" + k].reshape(64)) for k in "kvr"]
                                    + [twice(b) for b in i["L0_ffn_b1"]], 1)
    arrays["router"] = diag(i["L0_ffn_router_w"].T)
    arrays["moe_w"] = np.concatenate([diag(w) for k in ("w1", "w2") for w in i["L0_ffn_" + k]], 1)
    arrays["moe_b2"] = diag(i["L0_ffn_b2"])
    pick = np.zeros((16, 8, 128), f32)
    for e in range(8):
        pick[e, e, :64] = 1
        pick[8 + e, e, 64:] = 1
    arrays["pick"] = pick.reshape(16, 1024)
    arrays["rank_w"] = np.tile(np.arange(8, 0, -1).astype(f32), (128, 1))
    arrays["rk"] = np.concatenate([diag(i["L1_attn_W" + k]) for k in "kvr"], 1)
    arrays["wo"] = diag(i["L1_attn_Wo"])
    w = np.zeros((256, 256), f32)
    for u in range(256):
        w[u, u:] = i["L1_attn_time_w"][::-1][:256 - u]
    arrays["tw"] = np.ascontiguousarray(w.reshape(2, 128, 256).transpose(1, 0, 2).reshape(128, 512))
    arrays["tri"] = np.ascontiguousarray(np.triu(np.ones((256, 256), f32)).reshape(2, 128, 256).transpose(1, 0, 2).reshape(128, 512))
    slide = np.zeros((128, 60), f32)
    for g in range(4):
        slide[32 * g:32 * g + 32, 28 + g] = i["L0_attn_w_mlp"]
    arrays["slide"] = slide
    arrays["eye"] = np.eye(128, dtype=f32)

    arrays["edges"] = i["L1_ffn_edge_index"]
    arrays["w_gat"] = diag(i["L1_ffn_W_gat"])
    rows = [i["L1_ffn_" + n].reshape(16) for n in ("att_src", "att_dst", "b_gat", "ln_gamma", "ln_beta")]
    arrays["grow"] = np.tile(np.concatenate(rows), (128, 1))
    arrays["w1s"] = np.concatenate([np.concatenate([w, w], 0) for w in i["L1_ffn_W1"]], 1)
    arrays["w2s"] = np.concatenate(list(i["L1_ffn_W2"]), 1)
    arrays["f_b1"] = np.ascontiguousarray(i["L1_ffn_b1"].T)
    arrays["b2r"] = i["L1_ffn_b2"].reshape(1, 256)
    low = np.triu(np.ones((128, 128)), 1)
    arrays["cst"] = np.concatenate([np.eye(128), low, np.ones((128, 128)), np.zeros((128, 128))], 1).astype(np.float16)
    hf = np.zeros((128, 2, 128), f32)
    for j in range(2):
        hf[:64, j, 64 * j:64 * j + 64] = np.eye(64)
    arrays["half_f"] = hf.reshape(128, 256)

    nc = _bacc.Bacc("TRN2", target_bir_lowering=False, num_devices=1)
    t = {k: nc.dram_tensor("in_" + k, a.shape, _mybir.dt.from_np(a.dtype), kind="ExternalInput").ap() for k, a in arrays.items()}
    for n, (shape, dtype) in enumerate(_OUTS):
        t["out"] = nc.dram_tensor("out_0", shape, _mybir.dt.from_np(np.dtype(dtype)), kind="ExternalOutput").ap()
    audio_tower(nc, t)
    r = _run(nc, [{"in_" + k: a for k, a in arrays.items()}], core_ids=[0])
    return r.results[0]["out_0"]
```

```python
import concourse.bass as bass
from concourse import mybir
from contextlib import ExitStack

P = 128


def audio_tower(nc, t):
    f32 = mybir.dt.float32
    ALU = mybir.AluOpType
    ACT = mybir.ActivationFunctionType
    AX = mybir.AxisListType
    ds = bass.ds

    NB, L, D = 8, 256, 64
    COLS = NB * L
    CH = 512
    NCH = COLS // CH
    TILES = COLS // P
    STEPS = 8
    G = 2
    NG = 2 * G
    QT = 32
    TPP = L // QT
    NR = 16
    N_POOL = 6
    E = 8
    EPS = 1e-5
    BIG = 1e30
    E1, HEADS = 4, 4
    f16, i32 = mybir.dt.float16, mybir.dt.int32
    NE = 262144
    EPP = NE // P
    GEN = EPP
    M = 4096
    NQ = M // P
    COUNT_IN = 16
    HT = 32
    XC = 104
    XT = 2 * XC
    RC = 16
    WL = 192
    GR, GS = 4, 56
    QG = NQ // GR
    ARENA = 34200
    K_MAX, K_SUM = 26, 20

    ctx = ExitStack()
    with ctx:
        def sb(name, shape, dt=f32):
            return ctx.enter_context(nc.sbuf_tensor(name, shape, dt))

        def sem(name):
            return ctx.enter_context(nc.semaphore(name))

        ps = ctx.enter_context(nc.psum_tensor("ps", [P, 8, CH], f32))

        arena = sb("arena", [P, ARENA])
        off = [0]

        def carve(shape, dt=f32):
            n = 1
            for d in shape:
                n *= d
            words = n * (2 if dt == f16 else 4) // 4
            a = arena[:, off[0]:off[0] + words]
            off[0] += words
            assert off[0] <= ARENA, off[0]
            a = a if dt == f32 else a.bitcast(dt)
            names = "abcd"[:len(shape)]
            if len(shape) > 1:
                a = a.rearrange("p (%s) -> p %s" % (" ".join(names), " ".join(names)), **dict(zip(names, shape)))
            return a

        h, dev, sq, nrm = [carve([COLS]) for _ in range(4)]
        x_sb = carve([COLS])[0:8]
        wt_sb = sb("wt_sb", [8, 2 * P])
        w_sb = sb("w_sb", [P, t["wmat"].shape[1]])
        c_sb = sb("c_sb", [P, t["cols"].shape[1]])
        slide = sb("slide", [P, 60])
        eye = sb("eye", [P, P])
        dyn = sb("dyn", [P, 8])
        pool_kq = sb("pool_kq", [P, 2, L])
        g_paced = sem("g_paced")
        bias_q = sb("bias_q", [P, NB * TPP])
        g_w = sb("g_w", [P, 2])
        rstd_t = sb("rstd_t", [P, 2 * TILES])
        a_sb = carve([COLS])
        up = carve([2, NB, L + 2])
        dn = carve([2, NB, L + 2])
        AFTER_TOK = [off[0]]
        q_sb = a_sb
        k_sb = dn[:, :, :, :].rearrange("p a b l -> p (a b l)")[:, 0:COLS]
        nq_sb, nk_sb = dev, sq
        v_sb = carve([TILES, P])
        relu = carve([NR, L])
        maxes = arena[:, off[0]:off[0] + 2 * N_POOL * L].rearrange("p (t n l) -> p t n l", t=2, n=N_POOL)
        sc = sb("sc", [P, 2, L])
        st = sb("st", [P, 2, 4])
        vp = sb("vp", [P, 2, P])
        pT = sb("pT", [P, 2, 2, P])
        ao = sb("ao", [P, P])
        router = sb("router", [P, 16])
        moe_w = sb("moe_w", [P, 2, E, P])
        moe_b2 = sb("moe_b2", [16, P])
        pick = sb("pick", [16, E, P])
        rank_w = sb("rank_w", [P, E])
        lg, eq, s1, l2, s2 = [carve([2 * TILES, E]) for _ in range(5)]
        m1, mr = sb("m1", [P, 2 * TILES]), sb("mr", [P, 2 * TILES])
        cmbF = carve([COLS])[0:16]
        gbuf = carve([2, CH])
        gs = carve([2, CH])
        rk_raw = sb("rk_raw", [P, 3, P])
        rk_w = sb("rk_w", [P, 2, 3, P])
        wo_sb = sb("wo_sb", [P, P])
        omix = sb("omix", [P, 3])
        tw = sb("tw", [P, 2, L])
        tri = sb("tri", [P, 2, L])
        kT = carve([2, 2, P])
        kvT = carve([2, 2, P])
        sig = v_sb[:, :, :].rearrange("p t f -> p (t f)")
        rw = carve([2, 2, L])
        off[0] = 4 * COLS
        hg, num, gtmp = [carve([NQ, 16]) for _ in range(3)]
        a_self, a_dst, a_top, a_y, den, aliased = [carve([NQ, HEADS]) for _ in range(6)]
        e_small = carve([2, NQ, HEADS])
        pen, mu, rstd = [carve([NQ]) for _ in range(3)]
        hc, hct = carve([16]), carve([16])
        a_c = carve([HEADS])
        GATH_AT = [off[0]]
        gath = carve([GR * GS, 16])
        g_src = carve([GR * GS, HEADS])
        g_tmp = carve([GS, 16])
        pn = carve([GR, QG, GS])
        T1_AT = [off[0]]
        t1 = carve([HEADS, QG, GS])
        t2 = carve([4, QG, GS])
        g_top = carve([HEADS, QG])
        yb = carve([2 * TILES * E1, D])
        g1 = carve([2, CH])
        tl, te, t_1, t_l2, t_2 = [carve([2 * TILES, E1]) for _ in range(5)]
        tm1, tmr = carve([2 * TILES]), carve([2 * TILES])
        g2 = carve([2 * TILES, E1])
        outY = carve([TILES, 2, D])
        c_mask = arena[:, GATH_AT[0]:GATH_AT[0] + NQ * P].rearrange("p (q e) -> p q e", q=NQ)
        assert GATH_AT[0] + NQ * P <= T1_AT[0]
        c_pick = arena[:, COLS:COLS + NQ * P].rearrange("p (q e) -> p q e", q=NQ)
        c_diag = outY.rearrange("p t h f -> p (t h f)")[:, 0:6 * P].rearrange("p (r e) -> p r e", r=6)
        c_rhs = outY.rearrange("p t h f -> p (t h f)")[:, 6 * P:6 * P + NQ * 20].rearrange("p (q v) -> p q v", q=NQ)
        c_hot = outY.rearrange("p t h f -> p (t h f)")[:, 6 * P + NQ * 20:7 * P + NQ * 20]
        d_lo, d_hi = sb("d_lo", [P, EPP], f16), sb("d_hi", [P, EPP], f16)
        iota_x = sb("iota_x", [P, 64, HT], f16)[:, :, :]
        off[0] = COLS
        hot_lo = [carve([64, HT], f16) for _ in range(2)]
        hot_hi = [carve([64, HT], f16) for _ in range(2)]
        assert off[0] <= 3 * COLS
        off[0] = COLS
        e_src, e_dst, e_lo = [carve([EPP], i32) for _ in range(3)]
        assert off[0] <= 4 * COLS
        e_key = a_sb
        off[0] = AFTER_TOK[0]
        e_q, e_tmp = carve([EPP], i32), carve([EPP])
        off[0] = AFTER_TOK[0]
        hot = carve([XT, P], f16)
        off[0] = COLS
        slot_hot = [carve([2, WL], f16) for _ in range(4)]
        x_key = carve([XT])
        x_i, x_b, x_t1, x_t2 = [carve([XT], i32) for _ in range(4)]
        x_bf, x_A, x_B, x_new, x_run, x_rank, x_zero = [carve([XT]) for _ in range(7)]
        cnt_sb = carve([2, P], f16)
        off_sb = carve([2, P], f16)
        l_key, l_g, l_m = carve([WL]), carve([WL]), carve([WL])
        l_i = carve([GR * GS], i32)
        hot_off = carve([XT // RC, P], f16)
        assert off[0] <= 4 * COLS
        w_gat = sb("w_gat", [P, 32])
        grow = sb("grow", [P, 5, 16])
        w1s = sb("w1s", [P, E1, P])
        w2s = sb("w2s", [P, E1, D])
        f_b1 = sb("f_b1", [P, E1])
        b2r = sb("b2r", [1, E1, D])
        ones1 = sb("ones1", [1, P])
        table = nc.dram_tensor("gat_table", (M, 16), f32, kind="Internal").ap()
        q1f = sb("q1f", [P, GR * GS])
        table2 = nc.dram_tensor("gat_dst_table", (M, 8), f32, kind="Internal").ap()
        ones_sq = sb("ones_sq", [P, P])
        lane_id = sb("lane_id", [P, 1])
        idxQ = sb("idxQ", [P, NQ])
        flag = sb("flag", [P, 2])
        flag_i = sb("flag_i", [1, 1], i32)
        c_src, c_dst, c_lo, c_q, c_si, c_di = [sb(n, [P, 1], i32) for n in ("c_src", "c_dst", "c_lo", "c_q", "c_si", "c_di")]
        c_g, c_d = sb("c_g", [P, 16]), sb("c_d", [P, 8])
        c_f = sb("c_f", [P, 4])
        c_v = sb("c_v", [P, 6])
        c_t = sb("c_t", [P, 16])
        c_w = sb("c_w", [P, 2])
        c_e = sb("c_e", [P, 20])
        c_row = sb("c_row", [P, 2, P])
        c_top = sb("c_top", [P, NQ])
        c_tab = sb("c_tab", [P, NQ, 8])
        idx128 = sb("idx128", [P, P], f16)
        idxW = sb("idxW", [P, WL], f16)
        idxXT = sb("idxXT", [P, XT])
        cst = sb("cst", [P, 4, P], f16)
        half_f = sb("half_f", [P, 2, P])
        hsb = sb("hsb", [64, 2, 64])
        nd = sb("nd", [P, NQ])
        s_key = sb("s_key", [P, GR, GS])
        s_idx = sb("s_idx", [P, GR * GS], i32)
        bad = sb("bad", [P, 4])

        W = {n: w_sb[:, i * P:(i + 1) * P] for i, n in enumerate(
            ["tok2", "tok4", "q", "k", "v", "mean"])}
        C = {n: c_sb[:, i:i + 1] for i, n in enumerate(["b1", "b2", "b3", "b4", "b_mlp", "mixk", "mixv", "mixr"] + ["moe_b1_%d" % e for e in range(E)])}

        s_w = sem("weights_loaded")
        s_c = sem("edge_constants_loaded")
        s_x = sem("x_loaded")
        dve_done = sem("dve_done")
        recip_done = sem("recip_done")
        vp_ready = sem("vp_ready")
        bias_ready, tok_a, tok_mm, tok_relu, tok_out_mm, h_tok = [sem(n) for n in (
            "bias_ready", "tok_a", "tok_mm", "tok_relu", "tok_out_mm", "h_tok")]
        ln_mean, ln_dev, ln_sq, ln_var, ln_std, ln_rstd, ln_spread, ln_out = [
            sem("ln_" + n) for n in ("mean", "dev", "sq", "var", "std", "rstd", "spread", "out")]
        qk_mm, qk_copied, v_mm, v_copied = sem("qk_mm"), sem("qk_copied"), sem("v_mm"), sem("v_copied")
        relu_dve, relu_act, relu_used = sem("relu_dve"), sem("relu_act"), sem("relu_used")
        max_pool, bias_q_mm, kq_copied = sem("max_pool"), sem("bias_q_mm"), sem("kq_copied")
        score_read, max_ready, exp_ready, prob_ready = [sem(n) for n in (
            "score_read", "max_ready", "exp_ready", "prob_ready")]
        prob_T, pT_copied, pv_mm, ao_copied, ao_T, h_attn = [sem(n) for n in (
            "prob_T", "pT_copied", "pv_mm", "ao_copied", "ao_T", "h_attn")]
        lg_mm, ex_in, ex_done, cmb_ready, cmb_T, cmb_copied = [sem(n) for n in (
            "lg_mm", "ex_in", "ex_done", "cmb_ready", "cmb_T", "cmb_copied")]
        moe_hid, moe_bc, moe_gelu, moe_scaled, moe_used, moe_acc, h_moe = [sem(n) for n in (
            "moe_hid", "moe_bc", "moe_gelu", "moe_scaled", "moe_used", "moe_acc", "h_moe")]
        rk_scaled, rk_mm, rk_clip, rk_exp, rk_kv, rk_sums, rk_r, rk_sig, rk_gated, rk_y, h_rwkv = [sem(n) for n in (
            "rk_scaled", "rk_mm", "rk_clip", "rk_exp", "rk_kv", "rk_sums", "rk_r", "rk_sig", "rk_gated", "rk_y", "h_rwkv")]
        s_w2 = sem("late_weights_loaded")
        s_w3 = sem("last_weights_loaded")
        flag_in, flag_all, flag_ready, dve_tail, dve_live, gs_in, gs_out = [sem(n) for n in (
            "flag_in", "flag_all", "flag_ready", "dve_tail", "dve_live", "gs_in", "gs_out")]
        c_loaded, c_keyed, c_gathered, c_diagonal, c_rows, c_chain, c_tabled, c_table_written = [sem(n) for n in (
            "c_loaded", "c_keyed", "c_gathered", "c_diagonal", "c_rows", "c_chain", "c_tabled", "c_table_written")]
        c_free, c_paced, c_finished = sem("c_free"), sem("c_paced"), sem("c_finished")
        c_exp_in, c_exp_out, c_operands, c_summed = [sem(n) for n in ("c_exp_in", "c_exp_out", "c_operands", "c_summed")]
        gathered = [sem("gathered%d" % g) for g in range(GR)]
        gat_mm, hg_ready, hc_loaded, table_written, ge_in, ge_out, f_hid, f_gelu, f_out, f_copied, ones_ready = [sem(n) for n in (
            "gat_mm", "hg_ready", "hc_loaded", "table_written", "ge_in", "ge_out", "f_hid", "f_gelu", "f_out", "f_copied", "ones_ready")]
        outT_mm, outT_copied, s_out = sem("outT_mm"), sem("outT_copied"), sem("s_out")

        block = ctx.enter_context(nc.Block())
        out_v = t["out"].rearrange("(h b) l f -> h (b l) f", h=2).rearrange("h (t p) f -> p t h f", p=P)

        def ch(x, c):
            return x[:, c * CH:(c + 1) * CH]

        def seqs(x, k, c, off):
            return x[:, k, 2 * c:2 * c + 2, off:off + L]

        def seq_ps(b):
            return ps[:, b, :].rearrange("p (b l) -> p b l", b=2)

        LN_IN = [(h_tok, lambda c: c + 1), (h_attn, lambda c: 4 * (c + 1)), (h_moe, lambda c: c + 1),
                 (h_rwkv, lambda c: 2 * (c + 1))]

        def normed(k, c):
            return seqs(up, 0, c, 1) if k == 2 else ch(nrm, c)

        def cols2(x, k):
            return x.rearrange("p (b l) -> p b l", b=2) if k == 2 else x

        MAKER = "VAVGAVAVGVAVAGVAVAGVAVAGVVAVAGVV"
        ON_POOL = [e for e in range(QT) if MAKER[e] == "G"]
        N_ACT, N_DVE = MAKER.count("A"), MAKER.count("V")
        assert len(MAKER) == QT and {e % 4 for e in ON_POOL} == set(range(4))

        def query(e):
            return 8 * (e % 4) + e // 4

        def relu_free(eng, T, e):
            if isinstance(T, int):
                if T * QT + e - NR + 1 > 0:
                    eng.wait_ge(relu_used, T * QT + e - NR + 1)
            else:
                eng.wait_ge(relu_used, T * QT + (e - NR + 1))

        def wait(eng, s, v):
            if not isinstance(v, int) or v > 0:
                eng.wait_ge(s, v)

        e_loaded, e_hot, e_hot_used, e_hsb, e_nd_mm = [sem(n) for n in (
            "e_loaded", "e_hot", "e_hot_used", "e_hsb", "e_nd_mm")]
        x_hot, x_count, x_cnt, x_off, x_slot, x_slot_used, x_routed, e_iota, e_done = [sem(n) for n in (
            "x_hot", "x_count", "x_cnt", "x_off", "x_slot", "x_slot_used", "x_routed", "e_iota", "e_done")]

        def live_edges_by_column(dve):
            ts, tt, stt = nc.vector.tensor_scalar, nc.vector.tensor_tensor, nc.vector.scalar_tensor_tensor
            att_s = grow[:, 0, :]
            PER = [K_MAX, K_SUM]
            base = [0, GEN * K_MAX + 8]

            def chained(pas, t_):
                n = [0]

                def link(ins):
                    n[0] += 1
                    ins.then_inc(c_chain, 1)
                    dve.wait_ge(c_chain, t_ * PER[pas] + (base[pas] + n[0]))
                return link, n

            def decode(link, pas, t_):
                dve.wait_ge(c_loaded, (t_ + (1 + pas * GEN)) * 32)
                link(ts(c_lo[:, :], c_dst[:, :], P - 1, None, ALU.bitwise_and))
                link(ts(c_q[:, :], c_dst[:, :], 7, None, ALU.logical_shift_right))
                link(ts(c_f[:, 0:1], c_src[:, :], float(M - 1), None, ALU.is_lt))
                link(stt(c_f[:, 0:1], c_q[:, :], float(NQ), c_f[:, 0:1], ALU.is_lt, ALU.mult))
                link(stt(c_f[:, 1:2], c_lo[:, :], 1.0, c_f[:, 0:1], ALU.add, ALU.mult))
                link(ts(c_f[:, 1:2], c_f[:, 1:2], -1.0, None, ALU.add))
                link(nc.vector.tensor_copy(c_f[:, 2:3], c_q[:, :]))
                link(ts(c_di[:, :], c_dst[:, :], float(M - 1), None, ALU.min))
                ts(c_si[:, :], c_src[:, :], float(M - 1), None, ALU.min).then_inc(c_keyed, 1)
                dve.wait_ge(c_keyed, t_ + (1 + pas * GEN))
                nc.vector.memset(c_f[:, 3:4], 0.0).then_inc(c_free, 1)

            def source_scores(link, out_):
                link(tt(c_t[:, :], c_g[:, :], att_s, ALU.mult))
                link(nc.vector.reduce_sum(out_, c_t[:, :].rearrange("p (h e) -> p h e", h=HEADS), AX.X))

            nc.vector.memset(c_f[:, 3:4], 0.0).then_inc(c_free, 1)
            with dve.Fori(0, GEN) as t_:
                link, n = chained(0, t_)
                decode(link, 0, t_)
                dve.wait_ge(c_gathered, (t_ + 1) * 16)
                source_scores(link, c_v[:, 0:4])
                link(nc.vector.tensor_copy(c_v[:, 4:6], c_f[:, 1:3]))
                tt(c_diag, eye[:, :].unsqueeze(1).to_broadcast([P, 6, P]), c_v[:, :].unsqueeze(2).to_broadcast([P, 6, P]),
                   ALU.mult).then_inc(c_diagonal, 1)
                dve.wait_ge(c_rows, t_ + 1)
                link(ts(c_row[:, 0, :], ps[:, 1, P:2 * P], lane_id[:, 0:1], None, ALU.is_equal))
                for q_ in range(NQ):
                    ins = stt(c_mask[:, q_, :], ps[:, 1, 2 * P:3 * P], float(q_), c_row[:, 0, :], ALU.is_equal, ALU.mult)
                link(ins)
                cm = c_mask.rearrange("p q e -> p (q e)")
                link(ts(cm, cm, -1.0, BIG, ALU.add, ALU.mult))
                for hd in range(HEADS):
                    row = ps[:, hd // 3, (hd % 3) * P:(hd % 3 + 1) * P]
                    link(tt(c_pick, c_mask, row.unsqueeze(1).to_broadcast([P, NQ, P]), ALU.add))
                    link(nc.vector.reduce_max(c_top[:, :], c_pick, AX.X))
                    link(tt(a_top[:, :, hd], a_top[:, :, hd], c_top[:, :], ALU.max))
                assert n[0] == K_MAX, n[0]
            n = [GEN * K_MAX]

            def link(ins):
                n[0] += 1
                ins.then_inc(c_chain, 1)
                dve.wait_ge(c_chain, n[0])

            link(tt(a_y, a_top, a_dst, ALU.add))
            link(stt(a_top.rearrange("p q h -> p (q h)"), a_y.rearrange("p q h -> p (q h)"), 0.2,
                     a_y.rearrange("p q h -> p (q h)"), ALU.mult, ALU.max))
            link(nc.vector.memset(num, 0.0))
            link(nc.vector.memset(den, 0.0))
            link(nc.vector.tensor_copy(c_tab[:, :, 0:4], a_dst))
            link(nc.vector.tensor_copy(c_tab[:, :, 4:8], a_top))
            link(nc.vector.memset(c_top[:, :], 0.0))
            link(nc.vector.memset(c_t[:, :], 0.0))
            nc.vector.memset(c_row[:, 1, :], 0.0).then_inc(c_tabled, 1)
            with dve.Fori(0, GEN) as t_:
                link, n = chained(1, t_)
                decode(link, 1, t_)
                dve.wait_ge(c_gathered, t_ * 32 + (GEN * 16 + 32))
                source_scores(link, c_e[:, 0:4])
                e4 = c_e[:, 0:4]
                link(tt(e4, e4, c_d[:, 0:4], ALU.add))
                link(stt(e4, e4, 0.2, e4, ALU.mult, ALU.max))
                link(tt(e4, e4, c_d[:, 4:8], ALU.subtract))
                ts(e4, e4, 0.0, None, ALU.min).then_inc(c_exp_in, 1)
                dve.wait_ge(c_exp_out, t_ + 1)
                link(tt(c_e[:, 4:20].rearrange("p (h e) -> p h e", h=HEADS), c_g[:, :].rearrange("p (h e) -> p h e", h=HEADS),
                        e4.unsqueeze(2).to_broadcast([P, HEADS, 4]), ALU.mult))
                link(ts(c_top[:, :], idxQ[:, :], c_f[:, 2:3], None, ALU.is_equal))
                link(tt(c_rhs, c_top[:, :].unsqueeze(2).to_broadcast([P, NQ, 20]), c_e[:, :].unsqueeze(1).to_broadcast([P, NQ, 20]), ALU.mult))
                ts(c_hot, idx128[:, :], c_f[:, 1:2], None, ALU.is_equal).then_inc(c_operands, 1)
                dve.wait_ge(c_summed, t_ + 1)
                for j in range(2):
                    part = ps[:, j, 0:16 * 20].rearrange("p (q v) -> p q v", q=16)
                    qs = slice(16 * j, 16 * j + 16)
                    link(tt(den[:, qs, :], den[:, qs, :], part[:, :, 0:4], ALU.add))
                    link(tt(num[:, qs, :], num[:, qs, :], part[:, :, 4:20], ALU.add))
                assert n[0] == K_SUM, n[0]
            nc.vector.memset(c_f[:, 3:4], 0.0).then_inc(c_finished, 1)

        def attend_and_mix(dve, link):
            ts, tt, stt = nc.vector.tensor_scalar, nc.vector.tensor_tensor, nc.vector.scalar_tensor_tensor
            att_s, att_d, b_gat, gamma, beta = [grow[:, j, :] for j in range(5)]

            def nodes(x):
                return x.unsqueeze(1).to_broadcast([P, NQ, 16])

            def q4(x):
                return x.rearrange("p q (h e) -> p q h e", h=HEADS)

            def flat(x, s_="p q f -> p (q f)"):
                return x.rearrange(s_)

            for g in range(GR):
                for ql in range(QG):
                    link(ts(pn[:, g, ql, :], q1f[:, g * GS:(g + 1) * GS], float(g * QG + ql + 1), -1.0, ALU.is_equal, ALU.add))
            link(ts(flat(pn, "p g q w -> p (g q w)"), flat(pn, "p g q w -> p (g q w)"), BIG, None, ALU.mult))
            dve.wait_ge(s_w3, 6 * 16)
            dve.wait_ge(gat_mm, 1)
            nc.vector.tensor_copy(hg.rearrange("p (h t) f -> p t h f", h=2),
                                  ps[:, 7, :].rearrange("p (t h f) -> p t h f", t=TILES, h=2)).then_inc(hg_ready, 1)
            dve.wait_ge(hg_ready, 1)
            for a_, o_ in ((att_s, a_self), (att_d, a_dst)):
                link(tt(gtmp, hg, nodes(a_), ALU.mult))
                link(nc.vector.reduce_sum(o_, q4(gtmp), AX.X))
            for n in range(COUNT_1, EPP // HT):
                alias_hots(dve, n)
            dve.wait_ge(e_nd_mm, 1)
            link(nc.vector.tensor_copy(nd[:, :], ps[:, 5, 0:NQ]))
            link(ts(pen, nd[:, :], 0.0, -1.0, ALU.is_gt, ALU.add))
            link(ts(pen, pen, BIG, None, ALU.mult))
            dve.wait_ge(hc_loaded, 16)
            link(tt(hct, hc, att_s, ALU.mult))
            link(nc.vector.reduce_sum(a_c, hct.rearrange("p (h e) -> p h e", h=HEADS), AX.X))
            link(tt(aliased, pen.unsqueeze(2).to_broadcast([P, NQ, HEADS]), a_c.unsqueeze(1).to_broadcast([P, NQ, HEADS]), ALU.add))
            link(tt(a_top, a_self, aliased, ALU.max))
            dve.wait_ge(flag_ready, 1)
            over = dve.value_load(flag_i[0:1, 0:1], min_val=0, max_val=1)
            nl = [0]

            def link_live(ins):
                nl[0] += 1
                ins.then_inc(dve_live, 1)
                dve.wait_ge(dve_live, nl[0])

            with dve.If(over < 1):
                for g in range(GR):
                    G_ = gath[:, g * GS:(g + 1) * GS, :]
                    S_ = g_src[:, g * GS:(g + 1) * GS, :]
                    qs = slice(g * QG, (g + 1) * QG)
                    dve.wait_ge(gathered[g], 16 * GS)
                    link_live(tt(g_tmp, G_, att_s.unsqueeze(1).to_broadcast([P, GS, 16]), ALU.mult))
                    link_live(nc.vector.reduce_sum(S_, g_tmp.rearrange("p w (h e) -> p w h e", h=HEADS), AX.X))
                    link_live(tt(t1, S_.rearrange("p w h -> p h w").unsqueeze(2).to_broadcast([P, HEADS, QG, GS]),
                            pn[:, g, :, :].unsqueeze(1).to_broadcast([P, HEADS, QG, GS]), ALU.add))
                    link_live(nc.vector.reduce_max(g_top, t1, AX.X))
                    top = a_top[:, qs, :].rearrange("p q h -> p h q")
                    link_live(tt(top, top, g_top, ALU.max))
                    link_live(tt(a_y[:, qs, :], a_top[:, qs, :], a_dst[:, qs, :], ALU.add))
                    link_live(stt(a_top[:, qs, :], a_y[:, qs, :], 0.2, a_y[:, qs, :], ALU.mult, ALU.max))

                    def over_w(x):
                        return x[:, qs, :].rearrange("p q h -> p h q").unsqueeze(3).to_broadcast([P, HEADS, QG, GS])

                    link_live(tt(t1, t1, over_w(a_dst), ALU.add))
                    t1f = t1.rearrange("p h q w -> p (h q w)")
                    link_live(stt(t1f, t1f, 0.2, t1f, ALU.mult, ALU.max))
                    tt(t1, t1, over_w(a_top), ALU.subtract).then_inc(ge_in, 1)
                    dve.wait_ge(ge_out, g + 1)
                    link_live(nc.vector.reduce_sum(den[:, qs, :].rearrange("p q h -> p h q"), t1, AX.X))
                    for hd in range(HEADS):
                        link_live(tt(t2, t1[:, hd, :, :].unsqueeze(1).to_broadcast([P, 4, QG, GS]),
                                G_[:, :, 4 * hd:4 * hd + 4].rearrange("p w e -> p e w").unsqueeze(2).to_broadcast([P, 4, QG, GS]), ALU.mult))
                        link_live(nc.vector.reduce_sum(num[:, qs, 4 * hd:4 * hd + 4].rearrange("p q e -> p e q"), t2, AX.X))
            with dve.Else():
                live_edges_by_column(dve)
            nt = [0]

            def link_tail(ins):
                nt[0] += 1
                ins.then_inc(dve_tail, 1)
                dve.wait_ge(dve_tail, nt[0])

            link_tail(tt(e_small[:, 0, :, :], a_self, a_dst, ALU.add))
            link_tail(tt(e_small[:, 1, :, :], aliased, a_dst, ALU.add))
            ef = e_small.rearrange("p a q h -> p (a q h)")
            link_tail(stt(ef, ef, 0.2, ef, ALU.mult, ALU.max))
            link_tail(tt(e_small[:, 0, :, :], e_small[:, 0, :, :], a_top, ALU.subtract))
            tt(e_small[:, 1, :, :], e_small[:, 1, :, :], a_top, ALU.subtract).then_inc(gs_in, 1)
            dve.wait_ge(gs_out, 1)
            link_tail(tt(e_small[:, 1, :, :], e_small[:, 1, :, :], nd[:, :].unsqueeze(2).to_broadcast([P, NQ, HEADS]), ALU.mult))
            for j in range(2):
                e_ = e_small[:, j, :, :]
                link_tail(tt(den, den, e_, ALU.add))
                link_tail(tt(q4(gtmp), e_.unsqueeze(3).to_broadcast([P, NQ, HEADS, 4]), q4(hg) if j == 0 else q4(nodes(hc)), ALU.mult))
                link_tail(tt(num, num, gtmp, ALU.add))
            denf = den.rearrange("p q h -> p (q h)")
            link_tail(ts(denf, denf, 1e-16, None, ALU.add))
            link_tail(nc.vector.reciprocal(denf, denf))
            link_tail(tt(q4(num), q4(num), den.unsqueeze(3).to_broadcast([P, NQ, HEADS, 4]), ALU.mult))
            link_tail(tt(num, num, nodes(b_gat), ALU.add))
            link_tail(nc.vector.reduce_sum(mu, num, AX.X))
            link_tail(ts(mu, mu, 1 / 16, None, ALU.mult))
            link_tail(tt(num, num, mu.unsqueeze(2).to_broadcast([P, NQ, 16]), ALU.subtract))
            link_tail(tt(gtmp, num, num, ALU.mult))
            nc.vector.reduce_sum(mu, gtmp, AX.X).then_inc(gs_in, 1)
            dve.wait_ge(gs_out, 2)
            link_tail(nc.vector.reciprocal(rstd, mu))
            link_tail(tt(num, num, rstd.unsqueeze(2).to_broadcast([P, NQ, 16]), ALU.mult))
            link_tail(tt(num, num, nodes(gamma), ALU.mult))
            link_tail(tt(num, num, nodes(beta), ALU.add))
            link_tail(nc.vector.reduce_sum(tl, num.rearrange("p q (h e) -> p q e h", h=HEADS), AX.X))
            tlf = tl.rearrange("p q e -> p (q e)")
            link_tail(ts(tlf, tlf, 1 / HEADS, None, ALU.mult))

            def over_e1(x):
                return x.unsqueeze(2).to_broadcast([P, NQ, E1])

            ranks1 = rank_w[:, E - E1:E].unsqueeze(1).to_broadcast([P, NQ, E1])
            link_tail(nc.vector.reduce_max(tm1, tl, AX.X))
            tt(t_l2, tl, over_e1(tm1), ALU.subtract).then_inc(gs_in, 1)

            def first1(x, largest, pick_out):
                link_tail(tt(te, x, over_e1(largest), ALU.is_equal))
                link_tail(tt(te, te, ranks1, ALU.mult))
                link_tail(nc.vector.reduce_max(tmr, te, AX.X))
                link_tail(tt(pick_out, te, over_e1(tmr), ALU.is_equal))

            first1(tl, tm1, t_1)
            link_tail(stt(tl, t_1, -BIG, tl, ALU.mult, ALU.add))
            link_tail(nc.vector.reduce_max(tm1, tl, AX.X))
            first1(tl, tm1, t_2)
            link_tail(tt(t_1, t_1, t_2, ALU.add))
            dve.wait_ge(gs_out, 3)
            link_tail(tt(t_1, t_1, t_l2, ALU.mult))
            link_tail(nc.vector.reduce_sum(tm1, t_1, AX.X))
            link_tail(nc.vector.reciprocal(tm1, tm1))
            link_tail(tt(g2.rearrange("p (t h) e -> p t h e", h=2), t_1.rearrange("p (h t) e -> p t h e", h=2),
                    tm1.rearrange("p (h t) -> p t h", h=2).unsqueeze(3).to_broadcast([P, TILES, 2, E1]), ALU.mult))
            dve.wait_ge(f_copied, 32)
            link_tail(tt(yb, yb, g2.rearrange("p q e -> p (q e)").unsqueeze(2).to_broadcast([P, NQ * E1, D]), ALU.mult))
            link_tail(nc.vector.reduce_sum(outY.rearrange("p t h f -> p (t h) f"), yb.rearrange("p (q e) f -> p q f e", e=E1), AX.X))
            for j in range(4):
                dve.wait_ge(outT_mm, 4 * (j + 1))
                o_ = outY[:, 4 * j:4 * j + 4, :, :].rearrange("p t h f -> p (t h f)")
                tt(o_, o_, ps[:, j, :], ALU.add).then_inc(outT_copied, 1)

        def edges_dve(dve, link):
            ts, tt, stt = nc.vector.tensor_scalar, nc.vector.tensor_tensor, nc.vector.scalar_tensor_tensor
            dve.wait_ge(e_loaded, 32)
            ts(e_lo, e_dst, P - 1, None, ALU.bitwise_and)
            ts(e_q, e_dst, 7, None, ALU.logical_shift_right)
            link(ts(e_tmp, e_src, float(M - 1), None, ALU.is_lt))
            link(stt(e_tmp, e_q, float(NQ), e_tmp, ALU.is_lt, ALU.mult))
            link(stt(e_key, e_q, float(M), e_src, ALU.mult, ALU.add))
            link(stt(e_key, e_lo, float(NQ * M), e_key, ALU.mult, ALU.add))
            link(stt(e_key, e_key, 1.0, e_tmp, ALU.add, ALU.mult))
            link(stt(e_tmp, e_q, float(NQ), e_tmp, ALU.is_lt, ALU.subtract))
            ts(e_lo, e_dst, 63, None, ALU.bitwise_and)
            link(ts(e_q, e_dst, 6, None, ALU.logical_shift_right))
            ts(d_hi[:, :], e_q, 2048.0, None, ALU.min)
            link(stt(e_tmp, e_lo, 1.0, e_tmp, ALU.add, ALU.mult))
            link(ts(d_lo[:, :], e_tmp, -1.0, None, ALU.add))
            dve.wait_ge(e_iota, 6)
            for c in range(2):
                part = e_key[:, c * EPP // 2:(c + 1) * EPP // 2]
                for j in range(XC // 8):
                    k8 = x_key[:, c * XC + 8 * j:c * XC + 8 * j + 8]
                    link(nc.vector.max(k8, part))
                    link(nc.vector.match_replace(part, k8, part, 0.0))
            link(nc.vector.reduce_max(bad[:, 0:1], e_key, AX.X))
            link(ts(x_key, x_key, -1.0, None, ALU.add))
            link(nc.vector.tensor_copy(x_i, x_key))
            ts(x_b, x_i, 17, None, ALU.arith_shift_right)
            link(ts(x_t1, x_i, NQ * M - 1, None, ALU.bitwise_and))
            nc.vector.tensor_copy(x_bf, x_b)
            ts(x_t2, x_t1, 8, None, ALU.logical_shift_right)
            link(ts(x_t1, x_t1, 255, None, ALU.bitwise_and))
            ts(x_A, x_t2, 16.0, None, ALU.add)
            link(nc.vector.tensor_copy(x_B, x_t1))
            for t_ in range(XT):
                ins = ts(hot[:, t_, :], idx128[:, :], x_bf[:, t_:t_ + 1], None, ALU.is_equal)
                if t_ % 16 == 15:
                    ins.then_inc(x_hot, 1)
            link(nc.vector.memset(x_zero, 0.0))
            for c in range(2):
                a, b_ = c * XC, (c + 1) * XC
                link(nc.vector.memset(x_new[:, a:a + 1], 1.0))
                link(tt(x_new[:, a + 1:b_], x_bf[:, a + 1:b_], x_bf[:, a:b_ - 1], ALU.not_equal))
                link(tt(x_new[:, a:b_], x_new[:, a:b_], idxXT[:, a:b_], ALU.mult))
                link(nc.vector.tensor_tensor_scan(x_run[:, a:b_], x_zero[:, a:b_], x_new[:, a:b_], 0.0, ALU.max, ALU.max))
            link(tt(x_rank, idxXT[:, :], x_run, ALU.subtract))
            dve.wait_ge(x_count, 1)
            nc.vector.tensor_copy(cnt_sb, ps[:, 4:6, 0:P]).then_inc(x_cnt, 1)
            dve.wait_ge(x_off, 1)
            nc.vector.tensor_copy(off_sb[:, 0, :], ps[:, 6, 0:P])
            nc.vector.tensor_copy(off_sb[:, 1, :], ps[:, 7, 0:P])
            link(nc.vector.reduce_max(bad[:, 1:2], ps[:, 4, 0:P], AX.X))
            part = XT // RC
            for j in range(RC):
                a = j * part
                link(tt(hot_off, hot[:, a:a + part, :], off_sb[:, 2 * j // RC, :].unsqueeze(1).to_broadcast([P, part, P]), ALU.mult))
                link(nc.vector.reduce_sum(x_new[:, a:a + part], hot_off, AX.X))
            link(tt(x_rank, x_rank, x_new, ALU.add))
            for t_ in range(XT):
                if t_ >= 4:
                    dve.wait_ge(x_slot_used, t_ - 3)
                for j, x in enumerate((x_A, x_B)):
                    ins = ts(slot_hot[t_ % 4][:, j, :], idxW[:, :], x_rank[:, t_:t_ + 1], x[:, t_:t_ + 1], ALU.is_equal, ALU.mult)
                ins.then_inc(x_slot, 1)
            dve.wait_ge(x_routed, 1)
            link(nc.vector.tensor_copy(l_m, ps[:, 5, WL:2 * WL]))
            link(stt(l_key, ps[:, 5, 0:WL], 256.0, l_m, ALU.mult, ALU.add))
            for g in range(GR):
                lo, hi = M * (1 + g * QG), M * (1 + (g + 1) * QG)
                link(stt(l_m, l_key, float(lo), l_key, ALU.is_ge, ALU.mult))
                link(stt(l_g, l_key, float(hi), l_m, ALU.is_lt, ALU.mult))
                for j in range(GS // 8):
                    k8 = s_key[:, g, 8 * j:8 * j + 8]
                    link(nc.vector.max(k8, l_g))
                    link(nc.vector.match_replace(l_g, k8, l_g, 0.0))
                link(nc.vector.reduce_max(bad[:, 2 + (g > 0):3 + (g > 0)], l_g, AX.X))
                if g:
                    link(tt(bad[:, 2:3], bad[:, 2:3], bad[:, 3:4], ALU.max))
            link(ts(flag[:, 0:1], bad[:, 1:2], -float(WL), None, ALU.add))
            link(tt(flag[:, 0:1], flag[:, 0:1], bad[:, 0:1], ALU.max))
            tt(flag[:, 0:1], flag[:, 0:1], bad[:, 2:3], ALU.max).then_inc(flag_in, 1)
            dve.wait_ge(flag_all, 1)
            link(ts(flag[:, 1:2], flag[:, 1:2], 0.0, 1.0, ALU.max, ALU.min))
            nc.vector.tensor_copy(flag_i[:, :], flag[0:1, 1:2]).then_inc(flag_ready, 1)
            flat = s_key[:, :, :].rearrange("p g s -> p (g s)")
            link(nc.vector.tensor_copy(s_idx[:, :], flat))
            link(ts(l_i, s_idx[:, :], 12, None, ALU.logical_shift_right))
            nc.vector.tensor_copy(q1f[:, :], l_i)
            link(ts(s_idx[:, :], s_idx[:, :], M - 1, None, ALU.bitwise_and))

        COUNT_1 = NCH * E
        STEPS_C = (EPP // HT - COUNT_1) // COUNT_IN

        def alias_hots(dve, n):
            if n >= 2:
                dve.wait_ge(e_hot_used, n - 1)
            for dst, d in ((hot_lo[n % 2], d_lo), (hot_hi[n % 2], d_hi)):
                ins = nc.vector.tensor_tensor(dst, d[:, n * HT:(n + 1) * HT].unsqueeze(1).to_broadcast([P, 64, HT]),
                                              iota_x, ALU.is_equal)
            ins.then_inc(e_hot, 1)

        def count_aliases(pe, m):
            pe.wait_ge(e_hot, m + 1)
            for j in range(HT):
                ins = nc.tensor.matmul(ps[0:64, 6, 0:64], hot_lo[m % 2][:, :, j], hot_hi[m % 2][:, :, j],
                                       start=(m in (0, COUNT_1) and j == 0),
                                       stop=(m in (COUNT_1 - 1, EPP // HT - 1) and j == HT - 1))
            ins.then_inc(e_hot_used, 1)

        def edges_places(pe):
            mm = nc.tensor.matmul
            for t_ in range(XT):
                if t_ % 16 == 0:
                    pe.wait_ge(x_hot, t_ // 16 + 1)
                    if t_ == 0:
                        pe.wait_ge(e_iota, 6)
                ins = mm(ps[:, 4 + t_ // XC, 0:P], cst[:, 0, :], hot[:, t_, :], start=(t_ % XC == 0), stop=(t_ % XC == XC - 1))
            ins.then_inc(x_count, 1)
            pe.wait_ge(x_cnt, 1)
            LOW, ONES = cst[:, 1, :], cst[:, 2, :]
            mm(ps[:, 6, 0:P], LOW, cnt_sb[:, 0, :], start=True, stop=True)
            mm(ps[:, 7, 0:P], ONES, cnt_sb[:, 0, :], start=True, stop=False)
            mm(ps[:, 7, 0:P], LOW, cnt_sb[:, 1, :], start=False, stop=True)
            mm(ps[:, 4, 0:P], ONES, cnt_sb[:, 0, :], start=True, stop=False)
            mm(ps[:, 4, 0:P], ONES, cnt_sb[:, 1, :], start=False, stop=True).then_inc(x_off, 1)

        def edges_routes(pe):
            mm = nc.tensor.matmul
            for t_ in range(XT):
                pe.wait_ge(x_slot, t_ + 1)
                ins = mm(ps[:, 5, 0:2 * WL], hot[:, t_, :], slot_hot[t_ % 4].rearrange("p a b -> p (a b)"),
                         start=(t_ == 0), stop=(t_ == XT - 1))
                ins.then_inc(x_slot_used, 1)
            pe.wait_ge(x_slot_used, XT)
            mm(ps[0:32, 4, 256:257], eye[:, 0:32], eye[:, 0:1], start=True, stop=True).then_inc(x_routed, 1)

        def load_column(act, pas, t_):
            act.wait_ge(c_free, t_ + (pas * GEN + 1))
            for dst, k in ((c_src, 0), (c_dst, 1)):
                act.dma_start(dst[:, :], edge_cols[k][:, ds(t_, 1)], allow_slow_non_contiguous=True).then_inc(c_loaded, 16)

        edge_cols = t["edges"].rearrange("a (p k) -> a p k", p=P)

        def gather_live(pool):
            for w_ in range(GR * GS):
                nc.gpsimd.indirect_dma_start(gath[:, w_, :], None, table,
                                                 bass.IndirectOffsetOnAxis(ap=s_idx[:, w_:w_ + 1], axis=0)).then_inc(gathered[w_ // GS], 16)

        @block.gpsimd
        def _(pool):
            nc.gpsimd.iota(idx128[:, :], [[1, P]], base=0, channel_multiplier=0, allow_small_or_imprecise_dtypes=True).then_inc(e_iota, 1)
            nc.gpsimd.iota(idxW[:, :], [[1, WL]], base=0, channel_multiplier=0, allow_small_or_imprecise_dtypes=True).then_inc(e_iota, 1)
            nc.gpsimd.iota(idxXT[:, :], [[1, XT]], base=0, channel_multiplier=0, allow_small_or_imprecise_dtypes=True).then_inc(e_iota, 1)
            nc.gpsimd.iota(iota_x, [[1, 64], [0, HT]], base=0, channel_multiplier=0, allow_small_or_imprecise_dtypes=True).then_inc(e_iota, 1)

            nc.gpsimd.memset(c_w[:, :], 0.0).then_inc(c_paced, 1)
            nc.gpsimd.iota(lane_id[:, :], [[1, 1]], base=0, channel_multiplier=1, allow_small_or_imprecise_dtypes=True).then_inc(e_iota, 1)
            nc.gpsimd.iota(idxQ[:, :], [[1, NQ]], base=0, channel_multiplier=0, allow_small_or_imprecise_dtypes=True).then_inc(e_iota, 1)
            pool.wait_ge(flag_in, 1)
            nc.gpsimd.partition_all_reduce(flag[:, 1:2], flag[:, 0:1], P, bass.bass_isa.ReduceOp.max).then_inc(flag_all, 1)
            nc.gpsimd.memset(g_w[:, :], 0.0).then_inc(g_paced, 1)
            pool.wait_ge(qk_copied, 16)

            def pace(number):
                pool.wait_ge(g_paced, number)
                nc.gpsimd.tensor_tensor(g_w[:, 1:2], g_w[:, 0:1], g_w[:, 0:1], ALU.add).then_inc(g_paced, 1)

            def pair_of_batches(pair, first):
                done = 0 if first else pair * (TPP + 2) - 2
                if not first:
                    pool.wait_ge(max_pool, pair * (TPP * N_POOL))
                    pace(done)
                for j, x in enumerate((nk_sb, nq_sb)):
                    nc.gpsimd.tensor_copy(pool_kq[:, j, :], x[:, ds(pair * L, L)]).then_inc(kq_copied, 1)
                pool.wait_ge(kq_copied, pair * 2 + 2)
                pace(done + 1)
                for k in range(TPP):
                    T = pair * TPP + k
                    if not (first and k < 2):
                        pool.wait_ge(relu_used, T * QT - QT)
                        pace(done + 2 + (k - 2 if first else k))
                    for m, e in enumerate(ON_POOL):
                        nc.gpsimd.tensor_scalar(maxes[:, k % 2, m, :], pool_kq[:, 0, :],
                                                pool_kq[:, 1, k * QT + query(e):k * QT + query(e) + 1], None, ALU.max).then_inc(max_pool, 1)

            pair_of_batches(0, True)
            with pool.Fori(1, NB) as pair:
                pair_of_batches(pair, False)
            pool.wait_ge(e_done, 1)
            pool.wait_ge(flag_ready, 1)
            pool.wait_ge(table_written, 16)
            over = pool.value_load(flag_i[0:1, 0:1], min_val=0, max_val=1)
            with pool.If(over < 1):
                gather_live(pool)
            with pool.Else():
                with pool.Fori(0, GEN) as t_:
                    pool.wait_ge(c_paced, t_ + 1)
                    pool.wait_ge(c_keyed, t_ + 1)
                    nc.gpsimd.tensor_tensor(c_w[:, 1:2], c_w[:, 0:1], c_w[:, 0:1], ALU.add).then_inc(c_paced, 1)
                    nc.gpsimd.indirect_dma_start(c_g[:, :], None, table,
                                                 bass.IndirectOffsetOnAxis(ap=c_si[:, 0:1], axis=0)).then_inc(c_gathered, 16)
                pool.wait_ge(c_table_written, 16)
                with pool.Fori(0, GEN) as t_:
                    pool.wait_ge(c_paced, t_ + (GEN + 1))
                    pool.wait_ge(c_keyed, t_ + (GEN + 1))
                    nc.gpsimd.tensor_tensor(c_w[:, 1:2], c_w[:, 0:1], c_w[:, 0:1], ALU.add).then_inc(c_paced, 1)
                    nc.gpsimd.indirect_dma_start(c_g[:, :], None, table,
                                                 bass.IndirectOffsetOnAxis(ap=c_si[:, 0:1], axis=0)).then_inc(c_gathered, 16)
                    nc.gpsimd.indirect_dma_start(c_d[:, :], None, table2,
                                                 bass.IndirectOffsetOnAxis(ap=c_di[:, 0:1], axis=0)).then_inc(c_gathered, 16)

        @block.sync
        def _(sp):
            edge = t["edges"].rearrange("a (p k) -> a p k", p=P)
            sp.dma_start(c_sb[:, :], t["cols"]).then_inc(s_w, 16)
            sp.dma_start(slide[:, :], t["slide"]).then_inc(s_w, 16)
            sp.dma_start(x_sb[:, :], t["x"]).then_inc(s_x, 16)
            sp.dma_start(wt_sb[:, :], t["wtok"]).then_inc(s_x, 16)
            sp.dma_start(w_sb[:, :], t["wmat"]).then_inc(s_w, 16)
            sp.dma_start(e_src, edge[0]).then_inc(e_loaded, 16)
            sp.dma_start(e_dst, edge[1]).then_inc(e_loaded, 16)
            sp.dma_start(cst[:, :, :].rearrange("p a b -> p (a b)"), t["cst"]).then_inc(s_c, 16)
            sp.dma_start(half_f[:, :, :].rearrange("p a b -> p (a b)"), t["half_f"]).then_inc(s_c, 16)
            sp.dma_start(eye[:, :], t["eye"]).then_inc(s_c, 16)
            for dst, n in ((router[:, :], "router"), (moe_w[:, :, :, :].rearrange("p a e f -> p (a e f)"), "moe_w"),
                           (moe_b2[:, :], "moe_b2"),
                           (pick[:, :, :].rearrange("p e f -> p (e f)"), "pick"), (rank_w[:, :], "rank_w"),
                           (rk_raw[:, :, :].rearrange("p e f -> p (e f)"), "rk"), (wo_sb[:, :], "wo"),
                           (tw[:, :, :].rearrange("p k l -> p (k l)"), "tw"),
                           (tri[:, :, :].rearrange("p k l -> p (k l)"), "tri")):
                sp.dma_start(dst, t[n]).then_inc(s_w2, 16)
            for dst, n in ((w_gat[:, :], "w_gat"), (grow[:, :, :].rearrange("p a f -> p (a f)"), "grow"),
                           (w1s[:, :, :].rearrange("p e f -> p (e f)"), "w1s"),
                           (w2s[:, :, :].rearrange("p e f -> p (e f)"), "w2s"), (f_b1[:, :], "f_b1"),
                           (b2r[:, :, :].rearrange("p e f -> p (e f)"), "b2r")):
                sp.dma_start(dst, t[n]).then_inc(s_w3, 16)
            sp.wait_ge(hg_ready, 1)
            sp.dma_start(table.rearrange("(q p) f -> p q f", p=P), hg).then_inc(table_written, 16)
            sp.wait_ge(table_written, 16)
            sp.dma_start(hc, table[M - 1:M, :].to_broadcast([P, 16])).then_inc(hc_loaded, 16)
            sp.wait_ge(flag_ready, 1)
            over = sp.value_load(flag_i[0:1, 0:1], min_val=0, max_val=1)
            with sp.If(over < 1):
                sp.nop()
            with sp.Else():
                sp.wait_ge(c_tabled, 1)
                sp.dma_start(table2.rearrange("(q p) f -> p q f", p=P), c_tab[:, :, :]).then_inc(c_table_written, 16)
            sp.wait_ge(outT_copied, 4)
            for hh in range(2):
                sp.dma_start(out_v[:, :, hh, :], outY[:, :, hh, :]).then_inc(s_out, 16)
            sp.wait_ge(s_out, 32)

        @block.vector
        def _(dve):
            n = [0]

            def link(ins):
                n[0] += 1
                ins.then_inc(dve_done, 1)
                dve.wait_ge(dve_done, n[0])

            for x in (up, dn):
                for k in range(2):
                    nc.vector.memset(x[:, k, :, 0:1], 0.0)
                    nc.vector.memset(x[:, k, :, L + 1:L + 2], 0.0)
            nc.vector.memset(dyn[:, 3:4], EPS)
            nc.vector.memset(ones_sq[:, :], 1.0)
            nc.vector.memset(ones1[:, :], 1.0).then_inc(ones_ready, 1)
            dve.wait_ge(s_w, 48)
            nc.vector.tensor_tensor(dyn[:, 0:1], C["b1"], C["b2"], ALU.add)
            nc.vector.scalar_tensor_tensor(dyn[:, 1:2], C["b4"], 2.0, C["b3"], ALU.mult, ALU.add).then_inc(bias_ready, 1)
            dve.wait_ge(bias_ready, 1)
            edges_dve(dve, link)
            nc.vector.memset(dyn[:, 4:5], 0.0).then_inc(e_done, 1)

            def layernorm(k):
                for c in range(NCH):
                    dve.wait_ge(ln_mean, NCH * k + c + 1)
                    nc.vector.tensor_tensor(ch(dev, c), ch(h, c), ps[:, c, :], ALU.subtract).then_inc(ln_dev, 1)
                dve.wait_ge(ln_std, k + 1)
                nc.vector.reciprocal(rstd_t[:, :], rstd_t[:, :]).then_inc(ln_rstd, 1)
                for c in range(NCH):
                    dve.wait_ge(ln_spread, NCH * k + c + 1)
                    nc.vector.tensor_tensor(normed(k, c), cols2(ch(dev, c), k), cols2(ps[:, 4 + c, :], k), ALU.mult).then_inc(ln_out, 1)

            layernorm(0)
            for j in range(4):
                dve.wait_ge(v_mm, j + 1)
                nc.vector.tensor_copy(v_sb[:, 4 * j:4 * j + 4, :],
                                      ps[:, 4 + j, :].rearrange("p (t f) -> p t f", t=4)).then_inc(v_copied, 1)
            dve.wait_ge(qk_copied, 16)
            dve.wait_ge(bias_q_mm, 1)
            link(nc.vector.tensor_scalar(bias_q[:, :], ps[:, 5, 0:NB * TPP], C["b_mlp"], None, ALU.add))

            def softmax_max(T, par):
                dve.wait_ge(relu_used, T * QT + QT)
                nc.vector.tensor_scalar(sc[:, par, :], ps[:, par, 0:L], bias_q[:, ds(T, 1)], 0.0,
                                        ALU.add, ALU.max).then_inc(score_read, 1)
                dve.wait_ge(score_read, T + 1)
                nc.vector.reduce_max(st[:, par, 0:1], sc[:, par, :], AX.X, negate=True).then_inc(max_ready, 1)

            def softmax_scale(T, par):
                dve.wait_ge(exp_ready, T + 1)
                nc.vector.reciprocal(st[:, par, 2:3], st[:, par, 1:2]).then_inc(recip_done, 1)
                dve.wait_ge(recip_done, T + 1)
                nc.vector.tensor_scalar(sc[:, par, :], sc[:, par, :], st[:, par, 2:3], None,
                                        ALU.mult).then_inc(prob_ready, 1)

            def add_out(u):
                dve.wait_ge(ao_T, u + 1)
                hs = h[:, ds(u * P, P)]
                nc.vector.tensor_tensor(hs, hs, ps[:, 5, 0:P], ALU.add).then_inc(h_attn, 1)

            def pair_of_batches(pair, first):
                for k in range(TPP):
                    T = pair * TPP + k
                    last = not (first and k == 0)
                    for e in range(QT):
                        if MAKER[e] == "V":
                            relu_free(dve, T, e)
                            nc.vector.tensor_scalar(relu[:, e % NR, :], nk_sb[:, ds(pair * L, L)],
                                                    nq_sb[:, ds(pair * L + (k * QT + query(e)), 1)], 0.0,
                                                    ALU.subtract, ALU.max).then_inc(relu_dve, 1)
                        if e == 10 and last:
                            softmax_max(T - 1, (k + 1) % 2)
                        if e == 24 and last:
                            softmax_scale(T - 1, (k + 1) % 2)
                        if e == 6 and k % 4 == 3 and not (first and k == 3):
                            add_out(pair * 2 + (k // 4 - 1))

            pair_of_batches(0, True)
            with dve.Fori(1, NB) as pair:
                pair_of_batches(pair, False)
            softmax_max(NB * TPP - 1, 1)
            softmax_scale(NB * TPP - 1, 1)
            add_out(TILES - 1)

            layernorm(1)
            dve.wait_ge(s_w2, 9 * 16)
            NT = 2 * TILES

            def over_e(x):
                return x[:, :].unsqueeze(2).to_broadcast([P, NT, E])

            ranks = rank_w[:, :].unsqueeze(1).to_broadcast([P, NT, E])
            dve.wait_ge(lg_mm, 1)
            link(nc.vector.tensor_copy(lg[:, :, :].rearrange("p t e -> p (t e)"), ps[:, 7, 0:NT * E]))
            link(nc.vector.reduce_max(m1[:, :], lg[:, :, :], AX.X))
            nc.vector.tensor_tensor(l2[:, :, :], lg[:, :, :], over_e(m1), ALU.subtract).then_inc(ex_in, 1)

            def first_of_the_largest(x, largest, pick_out):
                link(nc.vector.tensor_tensor(eq[:, :, :], x[:, :, :], over_e(largest), ALU.is_equal))
                link(nc.vector.tensor_tensor(eq[:, :, :], eq[:, :, :], ranks, ALU.mult))
                link(nc.vector.reduce_max(mr[:, :], eq[:, :, :], AX.X))
                link(nc.vector.tensor_tensor(pick_out[:, :, :], eq[:, :, :], over_e(mr), ALU.is_equal))

            first_of_the_largest(lg, m1, s1)
            link(nc.vector.scalar_tensor_tensor(lg[:, :, :], s1[:, :, :], -BIG, lg[:, :, :], ALU.mult, ALU.add))
            link(nc.vector.reduce_max(m1[:, :], lg[:, :, :], AX.X))
            first_of_the_largest(lg, m1, s2)
            link(nc.vector.tensor_tensor(s1[:, :, :], s1[:, :, :], s2[:, :, :], ALU.add))
            dve.wait_ge(ex_done, 1)
            link(nc.vector.tensor_tensor(s1[:, :, :], s1[:, :, :], l2[:, :, :], ALU.mult))
            link(nc.vector.reduce_sum(m1[:, :], s1[:, :, :], AX.X))
            link(nc.vector.reciprocal(m1[:, :], m1[:, :]))
            nc.vector.tensor_tensor(s1[:, :, :], s1[:, :, :], over_e(m1), ALU.mult).then_inc(cmb_ready, 1)
            for c in range(NCH):
                dve.wait_ge(cmb_T, c + 1)
                nc.vector.tensor_copy(ch(cmbF, c), ps[0:16, c, :]).then_inc(cmb_copied, 1)
            for c in range(NCH):
                for e in range(E):
                    m = c * E + e
                    dve.wait_ge(moe_gelu, m + 1)
                    dve.wait_ge(moe_bc, m + 1)
                    wait(dve, moe_used, m - 1)
                    nc.vector.tensor_tensor(gs[:, m % 2, :], gbuf[:, m % 2, :], ps[:, 2 + m % 2, :],
                                            ALU.mult).then_inc(moe_scaled, 1)
                    alias_hots(dve, m)
                link(nc.vector.tensor_tensor(ch(h, c), ch(h, c), ch(nrm, c), ALU.add))
                dve.wait_ge(moe_acc, c + 1)
                nc.vector.tensor_tensor(ch(h, c), ch(h, c), ps[:, 4 + c % 2, :], ALU.add).then_inc(h_moe, 1)

            link(nc.vector.tensor_scalar(omix[:, :], c_sb[:, 5:8], -1.0, 1.0, ALU.mult, ALU.add))
            for j in range(3):
                nc.vector.tensor_scalar(rk_w[:, 0, j, :], rk_raw[:, j, :], c_sb[:, 5 + j:6 + j], None, ALU.mult)
                ins = nc.vector.tensor_scalar(rk_w[:, 1, j, :], rk_raw[:, j, :], omix[:, j:j + 1], None, ALU.mult)
            ins.then_inc(rk_scaled, 1)
            layernorm(2)

            def time_values(b):
                bank = ps[:, b % 4, :].rearrange("p (k w f) -> p k w f", k=2, w=2)
                dve.wait_ge(rk_mm, b + 1)
                wait(dve, rk_sums, b - 1)
                nc.vector.tensor_scalar(kT[:, b % 2, :, :], bank[:, :, 0, :], -60.0, 30.0,
                                        ALU.max, ALU.min).then_inc(rk_clip, 1)
                dve.wait_ge(rk_exp, b + 1)
                nc.vector.tensor_tensor(kvT[:, b % 2, :, :], kT[:, b % 2, :, :], bank[:, :, 1, :],
                                        ALU.mult).then_inc(rk_kv, 1)

            def gate(b):
                dve.wait_ge(rk_sums, b + 1)
                dve.wait_ge(rk_sig, b // 2 + 1)
                wait(dve, rk_y, b - 1)
                link(nc.vector.reciprocal(rw[:, b % 2, 0, :], ps[:, 4 + b % 2, 0:L]))
                link(nc.vector.tensor_tensor(rw[:, b % 2, 0, :], rw[:, b % 2, 0, :], ps[:, 4 + b % 2, L:2 * L], ALU.mult))
                nc.vector.tensor_tensor(rw[:, b % 2, 1, :], rw[:, b % 2, 0, :], sig[:, b * L:(b + 1) * L],
                                        ALU.mult).then_inc(rk_gated, 1)

            def add_y(b):
                dve.wait_ge(rk_y, b + 1)
                hs = h[:, b * L:(b + 1) * L]
                nc.vector.tensor_tensor(hs, hs, ps[:, 7, 0:L], ALU.add).then_inc(h_rwkv, 1)

            for b in range(NB + 2):
                if b < NB:
                    time_values(b)
                if 1 <= b <= NB:
                    gate(b - 1)
                if b >= 2:
                    add_y(b - 2)

            layernorm(3)
            attend_and_mix(dve, link)

        def copy_y(act, n):
            hh, c, e = n // (NCH * E1), n // E1 % NCH, n % E1
            act.wait_ge(f_out, n + 1)
            y = yb.rearrange("p (t h e) f -> p t h e f", h=2, e=E1)[:, 4 * c:4 * c + 4, hh, e, :]
            act.activation(y, ps[:, 2 + n % 2, 0:4 * D].rearrange("p (t f) -> p t f", t=4), ACT.Copy).then_inc(f_copied, 1)

        @block.scalar
        def _(act):
            act.wait_ge(bias_ready, 1)
            for c in range(NCH):
                act.wait_ge(tok_a, c + 1)
                for x in (up, dn):
                    act.activation(seqs(x, 0, c, 1), seq_ps(c), ACT.Relu, bias=dyn[:, 0:1]).then_inc(tok_relu, 1)
            for s in range(1, STEPS):
                for c in range(NCH):
                    for d, x in enumerate((up, dn)):
                        act.wait_ge(tok_mm, (s - 1) * 8 + 2 * c + d + 1)
                        act.activation(seqs(x, s % 2, c, 1), seq_ps((2 * c + d) % 4), ACT.Relu, bias=dyn[:, 0:1]).then_inc(tok_relu, 1)
            for c in range(NCH):
                act.wait_ge(tok_out_mm, c + 1)
                act.activation(ch(h, c), ps[:, c, :], ACT.Relu, bias=dyn[:, 1:2]).then_inc(h_tok, 1)

            def layernorm(k):
                for c in range(NCH):
                    act.wait_ge(ln_dev, NCH * k + c + 1)
                    act.activation(ch(sq, c), ch(dev, c), ACT.Square).then_inc(ln_sq, 1)
                act.wait_ge(ln_var, k + 1)
                act.activation(rstd_t[:, :], ps[:, 4, 0:2 * TILES], ACT.Sqrt, bias=dyn[:, 3:4]).then_inc(ln_std, 1)

            layernorm(0)
            for c in range(NCH):
                for d, (x, nx) in enumerate(((q_sb, nq_sb), (k_sb, nk_sb))):
                    act.wait_ge(qk_mm, 2 * c + d + 1)
                    act.activation(ch(x, c), ps[:, (2 * c + d) % 4, :], ACT.Copy).then_inc(qk_copied, 1)
                    act.activation(ch(nx, c), ps[:, (2 * c + d) % 4, :], ACT.Copy, scale=-1.0).then_inc(qk_copied, 1)
            act.wait_ge(qk_copied, 16)
            act.wait_ge(v_copied, 4)

            def softmax_exp(T, par):
                act.wait_ge(max_ready, T + 1)
                act.activation(sc[:, par, :], sc[:, par, :], ACT.Exp, bias=st[:, par, 0:1],
                               accum_out=st[:, par, 1:2]).then_inc(exp_ready, 1)

            def copy_pT(T, par):
                act.wait_ge(prob_T, T + 1)
                act.activation(pT[:, par, :, :].rearrange("p k j -> p (k j)"), ps[:, 4, 0:2 * P],
                               ACT.Copy).then_inc(pT_copied, 1)

            def copy_ao(u):
                act.wait_ge(pv_mm, 4 * u + 4)
                act.activation(ao[:, :], ps[:, 6, 0:P], ACT.Copy).then_inc(ao_copied, 1)

            def pair_of_batches(pair, first):
                for k in range(TPP):
                    T = pair * TPP + k
                    for e in range(QT):
                        if MAKER[e] == "A":
                            relu_free(act, T, e)
                            act.activation(relu[:, e % NR, :], k_sb[:, ds(pair * L, L)], ACT.Relu,
                                           bias=q_sb[:, ds(pair * L + (k * QT + query(e)), 1)],
                                           scale=-1.0).then_inc(relu_act, 1)
                        if e == 4 and not (first and k < 2):
                            copy_pT(T - 2, k % 2)
                        if e == 12 and k % 4 == 2 and not (first and k == 2):
                            copy_ao(pair * 2 + (k // 4 - 1))
                        if e == 14 and k == 2:
                            wait(act, pv_mm, pair * TPP)
                            act.activation(vp[:, :, :], v_sb[:, ds(pair * 2, 2), :], ACT.Copy).then_inc(vp_ready, 1)
                        if e == 16 and not (first and k == 0):
                            softmax_exp(T - 1, (k + 1) % 2)

            pair_of_batches(0, True)
            with act.Fori(1, NB) as pair:
                pair_of_batches(pair, False)
            T = NB * TPP
            copy_pT(T - 2, 0)
            softmax_exp(T - 1, 1)
            copy_pT(T - 1, 1)
            copy_ao(TILES - 1)

            layernorm(1)
            act.wait_ge(ex_in, 1)
            act.activation(l2[:, :, :], l2[:, :, :], ACT.Exp).then_inc(ex_done, 1)
            for m in range(NCH * E):
                act.wait_ge(moe_hid, m + 1)
                wait(act, moe_scaled, m - 1)
                act.activation(gbuf[:, m % 2, :], ps[:, m % 2, :], ACT.Gelu,
                               bias=C["moe_b1_%d" % (m % E)]).then_inc(moe_gelu, 1)
            act.wait_ge(e_hot_used, COUNT_1)
            act.activation(hsb[:, 0, :], ps[0:64, 6, 0:64], ACT.Copy).then_inc(e_hsb, 1)

            layernorm(2)
            for c in range(NCH):
                act.wait_ge(rk_r, c + 1)
                act.activation(ch(sig, c), ps[:, 6, :], ACT.Sigmoid).then_inc(rk_sig, 1)
            for b in range(NB):
                act.wait_ge(rk_clip, b + 1)
                act.activation(kT[:, b % 2, :, :], kT[:, b % 2, :, :], ACT.Exp).then_inc(rk_exp, 1)

            layernorm(3)
            act.wait_ge(s_w3, 6 * 16)
            for n in range(2 * NCH * E1):
                hh, c, e = n // (NCH * E1), n // E1 % NCH, n % E1
                act.wait_ge(f_hid, n + 1)
                wait(act, f_out, n - 1)
                act.activation(g1[:, n % 2, :], ps[:, n % 2, :], ACT.Gelu, bias=f_b1[:, e:e + 1]).then_inc(f_gelu, 1)
                if n:
                    copy_y(act, n - 1)
                if n == COUNT_IN + 1:
                    act.wait_ge(e_hot_used, EPP // HT)
                    act.activation(hsb[:, 1, :], ps[0:64, 6, 0:64], ACT.Copy).then_inc(e_hsb, 1)
            copy_y(act, 2 * NCH * E1 - 1)
            act.wait_ge(flag_ready, 1)
            over = act.value_load(flag_i[0:1, 0:1], min_val=0, max_val=1)
            with act.If(over < 1):
                for g in range(GR):
                    act.wait_ge(ge_in, g + 1)
                    act.activation(t1, t1, ACT.Exp).then_inc(ge_out, 1)
            with act.Else():
                with act.Fori(0, GEN) as t_:
                    load_column(act, 0, t_)
                with act.Fori(0, GEN) as t_:
                    load_column(act, 1, t_)
                    act.wait_ge(c_exp_in, t_ + 1)
                    act.activation(c_e[:, 0:4], c_e[:, 0:4], ACT.Exp).then_inc(c_exp_out, 1)
            act.wait_ge(gs_in, 1)
            act.activation(e_small, e_small, ACT.Exp).then_inc(gs_out, 1)
            act.wait_ge(gs_in, 2)
            act.activation(mu, mu, ACT.Sqrt, bias=dyn[:, 3:4], scale=1 / 16).then_inc(gs_out, 1)
            act.wait_ge(gs_in, 3)
            act.activation(t_l2, t_l2, ACT.Exp).then_inc(gs_out, 1)

        @block.tensor
        def _(pe):
            mm = nc.tensor.matmul
            pe.wait_ge(s_x, 32)
            for c in range(NCH):
                mm(ps[:, c, :], wt_sb[:, 0:P], ch(x_sb, c), start=True, stop=True).then_inc(tok_a, 1)
            pe.wait_ge(s_w, 48)
            for s in range(1, STEPS):
                for c in range(NCH):
                    for d, x in enumerate((up, dn)):
                        i = (s - 1) * 8 + 2 * c + d
                        b = i % 4
                        pe.wait_ge(tok_relu, i + 5 if i >= 4 else 2 * i + 2)
                        mm(ps[:, b, :], wt_sb[:, 0:P], ch(x_sb, c), start=True, stop=False)
                        mm(seq_ps(b), W["tok2"], seqs(x, (s - 1) % 2, c, 2 * d), start=False, stop=True).then_inc(tok_mm, 1)
                    if s == STEPS - 3 and c == 1:
                        pe.wait_ge(s_c, 48)
                        edges_places(pe)
            pe.wait_ge(tok_relu, STEPS * 8)
            for c in range(NCH):
                o = ps[:, c, :].rearrange("p (b l) -> p b l", b=2)
                mm(ps[:, c, :], wt_sb[:, P:2 * P], ch(x_sb, c), start=True, stop=False)
                mm(o, W["tok4"], seqs(up, (STEPS - 1) % 2, c, 0), start=False, stop=False)
                mm(o, W["tok4"], seqs(dn, (STEPS - 1) % 2, c, 2), start=False, stop=True).then_inc(tok_out_mm, 1)
            edges_routes(pe)
            pe.wait_ge(e_done, 1)

            def layernorm(k):
                for c in range(NCH):
                    pe.wait_ge(LN_IN[k][0], LN_IN[k][1](c))
                    mm(ps[:, c, :], W["mean"], ch(h, c), start=True, stop=True).then_inc(ln_mean, 1)
                for i in range(TILES):
                    pe.wait_ge(ln_sq, NCH * k + i // 4 + 1)
                    ins = mm(ps[:, 4, 2 * i:2 * i + 2], sq[:, i * P:(i + 1) * P], W["mean"][:, 0:D + 1:D], start=True, stop=True)
                ins.then_inc(ln_var, 1)
                pe.wait_ge(ln_rstd, k + 1)
                for c in range(NCH):
                    for i in range(4 * c, 4 * c + 4):
                        for hh in range(2):
                            ins = mm(ps[hh * D:(hh + 1) * D, 4 + c, (i % 4) * P:(i % 4 + 1) * P],
                                     rstd_t[:, 2 * i + hh:2 * i + hh + 1].to_broadcast([P, D]), eye[:, :], start=True, stop=True)
                    ins.then_inc(ln_spread, 1)

            layernorm(0)
            for c in range(NCH):
                pe.wait_ge(ln_out, c + 1)
                for d, w in enumerate(("q", "k")):
                    n = 2 * c + d
                    if n >= 4:
                        pe.wait_ge(qk_copied, 2 * (n - 4) + 2)
                    mm(ps[:, n % 4, :], W[w], ch(nrm, c), start=True, stop=True).then_inc(qk_mm, 1)
            for j in range(4):
                for i in range(4):
                    ins = mm(ps[:, 4 + j, i * P:(i + 1) * P], nrm[:, (4 * j + i) * P:(4 * j + i + 1) * P], W["v"],
                             start=True, stop=True)
                ins.then_inc(v_mm, 1)
            pe.wait_ge(qk_copied, 16)
            pe.wait_ge(v_copied, 4)
            for e in ON_POOL:
                j, r = e % 4, e // 4
                own = [x for x in ON_POOL if x % 4 == j]
                ins = mm(ps[32 * j:32 * j + 32, 5, 0:NB * TPP], slide[:, 28 - 4 * r:60 - 4 * r], q_sb[:, query(e)::QT],
                         start=(e == own[0]), stop=(e == own[-1]))
            ins.then_inc(bias_q_mm, 1)

            def scores(T, pair, k):
                wait(pe, score_read, T - 1)
                for e in range(QT):
                    tile = relu[:, e % NR, :]
                    if MAKER[e] == "A":
                        pe.wait_ge(relu_act, T * N_ACT + MAKER[:e + 1].count("A"))
                    elif MAKER[e] == "V":
                        pe.wait_ge(relu_dve, T * N_DVE + MAKER[:e + 1].count("V"))
                    else:
                        pe.wait_ge(max_pool, T * N_POOL + MAKER[:e + 1].count("G"))
                        tile = maxes[:, k % 2, ON_POOL.index(e), :]
                    j, r = e % 4, e // 4
                    ins = mm(ps[32 * j:32 * j + 32, k % 2, 0:L], slide[:, 28 - 4 * r:60 - 4 * r],
                             tile, start=(r == 0), stop=(r == 7))
                    ins.then_inc(relu_used, 1)

            def transposes(T, par):
                wait(pe, prob_ready, T + 1)
                wait(pe, pT_copied, T)
                for kb in range(2):
                    ins = nc.tensor.transpose(ps[:, 4, kb * P:(kb + 1) * P], sc[:, par, kb * P:(kb + 1) * P], eye[:, :])
                ins.then_inc(prob_T, 1)

            def values(T, pair, k):
                pe.wait_ge(pT_copied, T + 1)
                if k == 0:
                    pe.wait_ge(vp_ready, pair + 1)
                if k % 4 == 0:
                    wait(pe, ao_copied, T // 4 if isinstance(T, int) else pair * 2 + k // 4)
                s = k % 4
                for g in range(NG):
                    lo = (g // G) * D + g % G
                    for kb in range(2):
                        ins = mm(ps[32 * s:32 * s + 32, 6, lo:lo + D - 1:2], pT[:, k % 2, kb, g:P:NG],
                                 vp[:, kb, lo:lo + D - 1:2],
                                 start=(kb == 0), stop=(kb == 1))
                ins.then_inc(pv_mm, 1)

            def out_T(u):
                pe.wait_ge(ao_copied, u + 1)
                wait(pe, h_attn, u)
                nc.tensor.transpose(ps[:, 5, 0:P], ao[:, :], eye[:, :]).then_inc(ao_T, 1)

            def pair_of_batches(pair, first):
                for k in range(TPP):
                    T = pair * TPP + k
                    scores(T, pair, k)
                    if not (first and k == 0):
                        transposes(T - 1, (k + 1) % 2)
                    if not (first and k < 2):
                        values(T - 2, pair if k >= 2 else pair - 1, (k - 2) % TPP)
                    if k % 4 == 2 and not (first and k == 2):
                        out_T(pair * 2 + (k // 4 - 1))

            pair_of_batches(0, True)
            with pe.Fori(1, NB) as pair:
                pair_of_batches(pair, False)
            T = NB * TPP
            transposes(T - 1, 1)
            values(T - 2, NB - 1, TPP - 2)
            values(T - 1, NB - 1, TPP - 1)
            out_T(TILES - 1)

            layernorm(1)
            pe.wait_ge(s_w2, 9 * 16)
            pe.wait_ge(ln_out, NCH * 2)
            for i in range(TILES):
                ins = mm(ps[:, 7, i * 16:(i + 1) * 16], nrm[:, i * P:(i + 1) * P], router[:, :], start=True, stop=True)
            ins.then_inc(lg_mm, 1)
            pe.wait_ge(cmb_ready, 1)
            for i in range(TILES):
                ins = nc.tensor.transpose(ps[0:16, i // 4, (i % 4) * P:(i % 4 + 1) * P],
                                          s1[:, 2 * i:2 * i + 2, :].rearrange("p h e -> p (h e)"), eye[:, :])
                if i % 4 == 3:
                    ins.then_inc(cmb_T, 1)

            def expert_out(m):
                c, e = m // E, m % E
                pe.wait_ge(moe_scaled, m + 1)
                if e == 0:
                    wait(pe, h_moe, c - 1)
                mm(ps[:, 4 + c % 2, :], moe_w[:, 1, e, :], gs[:, m % 2, :], start=(e == 0), stop=False).then_inc(moe_used, 1)
                if e == E - 1:
                    mm(ps[:, 4 + c % 2, :], moe_b2[:, :], ch(cmbF, c), start=False, stop=True).then_inc(moe_acc, 1)

            pe.wait_ge(cmb_copied, NCH)
            for m in range(NCH * E):
                c, e = m // E, m % E
                wait(pe, moe_gelu, m - 1)
                mm(ps[:, m % 2, :], moe_w[:, 0, e, :], ch(nrm, c), start=True, stop=True).then_inc(moe_hid, 1)
                wait(pe, moe_scaled, m - 1)
                mm(ps[:, 2 + m % 2, :], pick[:, e, :], ch(cmbF, c), start=True, stop=True).then_inc(moe_bc, 1)
                if m:
                    expert_out(m - 1)
                    count_aliases(pe, m - 1)
            expert_out(NCH * E - 1)
            count_aliases(pe, NCH * E - 1)
            pe.wait_ge(e_hsb, 1)

            layernorm(2)
            pe.wait_ge(ln_out, NCH * 3)
            pe.wait_ge(rk_scaled, 1)

            def keys_values(b):
                wait(pe, rk_kv, b - 3)
                for kb in range(2):
                    for prev in range(2):
                        o = 1 - prev + kb * P
                        ins = mm(ps[:, b % 4, kb * 2 * P:(kb + 1) * 2 * P], up[:, 0, b, o:o + P],
                                 rk_w[:, prev, 0:2, :].rearrange("p w f -> p (w f)"), start=(prev == 0), stop=(prev == 1))
                ins.then_inc(rk_mm, 1)

            def receptance(c):
                wait(pe, rk_sig, c)
                for prev in range(2):
                    ins = mm(seq_ps(6), rk_w[:, prev, 2, :], seqs(up, 0, c, 1 - prev), start=(prev == 0), stop=(prev == 1))
                ins.then_inc(rk_r, 1)

            def sums(b):
                pe.wait_ge(rk_kv, b + 1)
                wait(pe, rk_gated, b - 1)
                for j, (x, w) in enumerate(((kT, tri), (kvT, tw))):
                    for kb in range(2):
                        ins = mm(ps[:, 4 + b % 2, j * L:(j + 1) * L], x[:, b % 2, kb, :], w[:, kb, :],
                                 start=(kb == 0), stop=(kb == 1))
                ins.then_inc(rk_sums, 1)

            def project(b):
                pe.wait_ge(rk_gated, b + 1)
                wait(pe, h_rwkv, b)
                mm(ps[:, 7, 0:L], wo_sb[:, :], rw[:, b % 2, 1, :], start=True, stop=True).then_inc(rk_y, 1)

            for c in range(NCH):
                receptance(c)
            for b in range(NB + 2):
                if b < NB:
                    keys_values(b)
                if 1 <= b <= NB:
                    sums(b - 1)
                if b >= 2:
                    project(b - 2)

            layernorm(3)
            pe.wait_ge(ln_out, NCH * 4)
            pe.wait_ge(s_w3, 6 * 16)
            pe.wait_ge(ones_ready, 1)
            for i in range(TILES):
                ins = mm(ps[:, 7, i * 32:(i + 1) * 32], nrm[:, i * P:(i + 1) * P], w_gat[:, :], start=True, stop=True)
            ins.then_inc(gat_mm, 1)

            def expert(n):
                e = n % E1
                wait(pe, f_copied, n - 1)
                mm(ps[:, 2 + n % 2, 0:4 * D].rearrange("p (t f) -> p t f", t=4), ones1[:, :],
                   b2r[:, e, :].unsqueeze(1).to_broadcast([1, 4, D]), start=True, stop=False)
                pe.wait_ge(f_gelu, n + 1)
                for j in range(4):
                    ins = mm(ps[:, 2 + n % 2, j * D:(j + 1) * D], g1[:, n % 2, j * P:(j + 1) * P], w2s[:, e, :],
                             start=False, stop=(j == 3))
                ins.then_inc(f_out, 1)

            for n in range(2 * NCH * E1):
                hh, c, e = n // (NCH * E1), n // E1 % NCH, n % E1
                wait(pe, f_gelu, n - 1)
                half = slice(hh * D, hh * D + D)
                mm(ps[:, n % 2, :], w1s[half, e, :], nrm[half, c * CH:(c + 1) * CH], start=True, stop=True).then_inc(f_hid, 1)
                if n:
                    expert(n - 1)
                if n < COUNT_IN:
                    for m in range(STEPS_C):
                        count_aliases(pe, COUNT_1 + n * STEPS_C + m)
                if n == COUNT_IN + 2:
                    pe.wait_ge(e_hsb, 2)
                    for part in range(2):
                        for j in range(2):
                            ins = mm(ps[:, 5, 0:NQ], half_f[0:64, j, :], hsb[:, part, j::2],
                                     start=(part == 0 and j == 0), stop=(part == 1 and j == 1))
                    ins.then_inc(e_nd_mm, 1)
            expert(2 * NCH * E1 - 1)
            pe.wait_ge(f_copied, 2 * NCH * E1)
            pe.wait_ge(flag_ready, 1)
            over = pe.value_load(flag_i[0:1, 0:1], min_val=0, max_val=1)
            with pe.If(over < 1):
                pe.nop()
            with pe.Else():
                with pe.Fori(0, GEN) as t_:
                    pe.wait_ge(c_diagonal, t_ + 1)
                    for j in range(2):
                        ins = mm(ps[:, j, 0:3 * P], ones_sq[:, :], c_diag[:, 3 * j:3 * j + 3, :].rearrange("p r e -> p (r e)"),
                                 start=True, stop=True)
                    ins.then_inc(c_rows, 1)
                with pe.Fori(0, GEN) as t_:
                    pe.wait_ge(c_operands, t_ + 1)
                    for j in range(2):
                        ins = mm(ps[:, j, 0:16 * 20], c_hot, c_rhs[:, 16 * j:16 * j + 16, :].rearrange("p q v -> p (q v)"),
                                 start=True, stop=True)
                    ins.then_inc(c_summed, 1)
                pe.wait_ge(c_finished, 1)

            pe.wait_ge(h_rwkv, NB)
            for i in range(TILES):
                nc.tensor.transpose(ps[:, i // 4, (i % 4) * P:(i % 4 + 1) * P], h[:, i * P:(i + 1) * P],
                                    eye[:, :]).then_inc(outT_mm, 1)


_OUTS = [((16, 256, 64), "float32")]


def kernel(**inputs):
    import numpy as np
    import concourse.bacc as _bacc
    from concourse import mybir as _mybir
    from concourse.bass_utils import run_bass_kernel_spmd as _run

    i = {k: np.ascontiguousarray(v) for k, v in inputs.items()}
    f32 = np.float32

    def diag(w):
        a, b = w.shape
        o = np.zeros((2 * a, 2 * b), f32)
        o[:a, :b] = w
        o[a:, b:] = w
        return o

    def twice(v):
        return np.concatenate([v, v]).reshape(128, 1)

    arrays = {}
    arrays["x"] = np.ascontiguousarray(i["x"].reshape(2, 8, 4, 256).transpose(0, 2, 1, 3).reshape(8, 2048))
    arrays["wtok"] = np.concatenate([diag(i["L0_tok_W1"].T), diag(i["L0_tok_W3"].T)], 1)
    mean = diag(np.full((64, 64), 1 / 64, f32))
    arrays["wmat"] = np.concatenate([
        diag(i["L0_tok_W2"].T), diag(i["L0_tok_W4"].T), diag(i["L0_attn_Wq"].T), diag(i["L0_attn_Wk"].T),
        diag(i["L0_attn_Wv"].T), mean], 1)
    arrays["cols"] = np.concatenate([twice(i["L0_tok_b%d" % k]) for k in (1, 2, 3, 4)]
                                    + [np.full((128, 1), i["L0_attn_b_mlp"][0], f32)]
                                    + [twice(i["L1_attn_time_mix_" + k].reshape(64)) for k in "kvr"]
                                    + [twice(b) for b in i["L0_ffn_b1"]], 1)
    arrays["router"] = diag(i["L0_ffn_router_w"].T)
    arrays["moe_w"] = np.concatenate([diag(w) for k in ("w1", "w2") for w in i["L0_ffn_" + k]], 1)
    arrays["moe_b2"] = diag(i["L0_ffn_b2"])
    pick = np.zeros((16, 8, 128), f32)
    for e in range(8):
        pick[e, e, :64] = 1
        pick[8 + e, e, 64:] = 1
    arrays["pick"] = pick.reshape(16, 1024)
    arrays["rank_w"] = np.tile(np.arange(8, 0, -1).astype(f32), (128, 1))
    arrays["rk"] = np.concatenate([diag(i["L1_attn_W" + k]) for k in "kvr"], 1)
    arrays["wo"] = diag(i["L1_attn_Wo"])
    w = np.zeros((256, 256), f32)
    for u in range(256):
        w[u, u:] = i["L1_attn_time_w"][::-1][:256 - u]
    arrays["tw"] = np.ascontiguousarray(w.reshape(2, 128, 256).transpose(1, 0, 2).reshape(128, 512))
    arrays["tri"] = np.ascontiguousarray(np.triu(np.ones((256, 256), f32)).reshape(2, 128, 256).transpose(1, 0, 2).reshape(128, 512))
    slide = np.zeros((128, 60), f32)
    for g in range(4):
        slide[32 * g:32 * g + 32, 28 + g] = i["L0_attn_w_mlp"]
    arrays["slide"] = slide
    arrays["eye"] = np.eye(128, dtype=f32)

    arrays["edges"] = i["L1_ffn_edge_index"]
    arrays["w_gat"] = diag(i["L1_ffn_W_gat"])
    rows = [i["L1_ffn_" + n].reshape(16) for n in ("att_src", "att_dst", "b_gat", "ln_gamma", "ln_beta")]
    arrays["grow"] = np.tile(np.concatenate(rows), (128, 1))
    arrays["w1s"] = np.concatenate([np.concatenate([w, w], 0) for w in i["L1_ffn_W1"]], 1)
    arrays["w2s"] = np.concatenate(list(i["L1_ffn_W2"]), 1)
    arrays["f_b1"] = np.ascontiguousarray(i["L1_ffn_b1"].T)
    arrays["b2r"] = i["L1_ffn_b2"].reshape(1, 256)
    low = np.triu(np.ones((128, 128)), 1)
    arrays["cst"] = np.concatenate([np.eye(128), low, np.ones((128, 128)), np.zeros((128, 128))], 1).astype(np.float16)
    hf = np.zeros((128, 2, 128), f32)
    for j in range(2):
        hf[:64, j, 64 * j:64 * j + 64] = np.eye(64)
    arrays["half_f"] = hf.reshape(128, 256)

    nc = _bacc.Bacc("TRN2", target_bir_lowering=False, num_devices=1)
    t = {k: nc.dram_tensor("in_" + k, a.shape, _mybir.dt.from_np(a.dtype), kind="ExternalInput").ap() for k, a in arrays.items()}
    for n, (shape, dtype) in enumerate(_OUTS):
        t["out"] = nc.dram_tensor("out_0", shape, _mybir.dt.from_np(np.dtype(dtype)), kind="ExternalOutput").ap()
    audio_tower(nc, t)
    r = _run(nc, [{"in_" + k: a for k, a in arrays.items()}], core_ids=[0])
    return r.results[0]["out_0"]
```
